# Optimizing a Trainium2 kernel written in Bass

```python
import numpy as np
import jax
import jax.numpy as jnp

def _softmax(x, axis=-1):
    return jax.nn.softmax(x, axis=axis)

def _gelu(x):
    return jax.nn.gelu(x, approximate=True)

def _silu(x):
    return jax.nn.silu(x)

def _sigmoid(x):
    return jax.nn.sigmoid(x)

def _layernorm(x, axis=-1, eps=1e-05):
    m = jnp.mean(x, axis=axis, keepdims=True)
    v = jnp.var(x, axis=axis, keepdims=True)
    return (x - m) / jnp.sqrt(v + eps)

def _scatter_add(tgt, idx, src, axis=0):
    return tgt.at[idx].add(src)

def _segment_sum(src, seg, n):
    return jax.ops.segment_sum(src, seg, n)
kernel_name = 'mk_pixart_seq_d2_seqx_r4_8c5ebe'

def setup_inputs(seed: int=0):
    np.random.seed(seed)
    _w = jnp.asarray

    def _rec_inputs():
        import jax
        import jax.numpy as jnp
        _rk = jax.random.key(seed)
        x = -0.0002928 + 1 * jax.random.normal(jax.random.fold_in(_rk, 1), (32, 100, 256), jnp.float32)
        _lenS = 100 - jax.random.randint(jax.random.fold_in(_rk, 7), (32,), 0, max(1, 100 // 4) + 1, jnp.int32)
        _lenS2 = 361 - jax.random.randint(jax.random.fold_in(_rk, 8), (32,), 0, max(1, 361 // 4) + 1, jnp.int32)
        cond_1024 = 0.0061147 + 1.02565 * jax.random.normal(jax.random.fold_in(_rk, 11), (32, 256), jnp.float32)
        _ctx_768P = jax.random.normal(jax.random.fold_in(_rk, 12), (32, 16, 192), jnp.float32)
        _ctx_768c = jax.random.dirichlet(jax.random.fold_in(_rk, 512), 0.3 * jnp.ones((16,), jnp.float32), (32, 361))
        _ctx_768t = jnp.einsum('bsk,bkd->bsd', _ctx_768c, _ctx_768P)
        _ctx_768t = _ctx_768t * jax.lax.rsqrt(jnp.mean(jnp.square(_ctx_768t)) + 1e-12) * 0.953939
        ctx_768 = -0.00284796 + 0.998162 * (_ctx_768t + 0.3 * jax.random.normal(jax.random.fold_in(_rk, 612), (32, 361, 192), jnp.float32))
        return (x, cond_1024, ctx_768)
    x, cond_1024, ctx_768 = _rec_inputs()

    def _L0_xcond_setup():
        import jax, jax.numpy as jnp
        import numpy as np
        B, N, D, H, TD, TL = (4, 256, 256, 16, 192, 77)
        HD = D // H
        EPS = 1e-06

        def _ln(x):
            mu = jnp.mean(x, axis=-1, keepdims=True)
            var = jnp.var(x, axis=-1, keepdims=True)
            return (x - mu) * jax.lax.rsqrt(var + EPS)

        def _modulate(x, shift, scale):
            return x * (1.0 + scale[:, None, :]) + shift[:, None, :]

        def _heads(t):
            return t.reshape(t.shape[0], t.shape[1], H, HD).transpose(0, 2, 1, 3)

        def _attend(q, k, v):
            sim = jnp.einsum('bhid,bhjd->bhij', q, k) * HD ** (-0.5)
            attn = jax.nn.softmax(sim, axis=-1)
            out = jnp.einsum('bhij,bhjd->bhid', attn, v)
            return out.transpose(0, 2, 1, 3).reshape(out.shape[0], -1, D)
        key = jax.random.key(seed)
        ks = jax.random.split(key, 16)
        s = 0.02
        return {'x': jax.random.normal(ks[0], (B, N, D), jnp.float32), 'c': jax.random.normal(ks[1], (B, D), jnp.float32), 'text_embed': jax.random.normal(ks[2], (B, TL, TD), jnp.float32), 'W_ada': jax.random.normal(ks[3], (D, 6 * D), jnp.float32) * s, 'b_ada': jnp.zeros((6 * D,), jnp.float32), 'W_qkv': jax.random.normal(ks[4], (D, 3 * D), jnp.float32) * s, 'b_qkv': jnp.zeros((3 * D,), jnp.float32), 'W_proj': jax.random.normal(ks[5], (D, D), jnp.float32) * s, 'b_proj': jnp.zeros((D,), jnp.float32), 'W_ctx': jax.random.normal(ks[6], (TD, D), jnp.float32) * s, 'b_ctx': jnp.zeros((D,), jnp.float32), 'W_q': jax.random.normal(ks[7], (D, D), jnp.float32) * s, 'W_k': jax.random.normal(ks[8], (D, D), jnp.float32) * s, 'W_v': jax.random.normal(ks[9], (D, D), jnp.float32) * s, 'W_out': jax.random.normal(ks[10], (D, D), jnp.float32) * s, 'b_out': jnp.zeros((D,), jnp.float32), 'W_fc1': jax.random.normal(ks[11], (D, 4 * D), jnp.float32) * s, 'b_fc1': jnp.zeros((4 * D,), jnp.float32), 'W_fc2': jax.random.normal(ks[12], (4 * D, D), jnp.float32) * s, 'b_fc2': jnp.zeros((D,), jnp.float32)}
    _L0_xcond_all = _L0_xcond_setup()
    _L0_xcond_in = {k: v for k, v in _L0_xcond_all.items() if k in ('W_ada', 'b_ada', 'W_qkv', 'b_qkv', 'W_proj', 'b_proj', 'W_ctx', 'b_ctx', 'W_q', 'W_k', 'W_v', 'W_out', 'b_out', 'W_fc1', 'b_fc1', 'W_fc2', 'b_fc2')}
    del _L0_xcond_all

    def _L1_xcond_setup():
        import jax, jax.numpy as jnp
        import numpy as np
        B, N, M = (2, 256, 128)
        D, H, DH = (256, 16, 64)
        MID = H * DH
        DC = 192
        MULT = 4
        EPS = 1e-05

        def _ln(x, w, b):
            mu = jnp.mean(x, -1, keepdims=True)
            var = jnp.mean((x - mu) ** 2, -1, keepdims=True)
            return (x - mu) * jax.lax.rsqrt(var + EPS) * w + b

        def _sincos(n, d):
            inv = 1.0 / 10000.0 ** (jnp.arange(0, d, 2, dtype=jnp.float32) / d)
            ang = jnp.arange(n, dtype=jnp.float32)[:, None] * inv[None, :]
            return (jnp.sin(ang), jnp.cos(ang))

        def _rope(x, sin, cos):
            s = sin[None, None]
            c = cos[None, None]
            xe = x[..., ::2]
            xo = x[..., 1::2]
            re = xe * c - xo * s
            ro = xe * s + xo * c
            return jnp.stack((re, ro), axis=-1).reshape(x.shape)

        def _heads(t):
            b, n, _ = t.shape
            return t.reshape(b, n, H, DH).transpose(0, 2, 1, 3)

        def _attn(xq, ctx, wq, wkv, wo, bo):
            q = _heads(xq @ wq)
            k, v = jnp.split(ctx @ wkv, 2, axis=-1)
            k = _heads(k)
            v = _heads(v)
            sq, cq = _sincos(q.shape[2], DH)
            sk, ck = _sincos(k.shape[2], DH)
            q = _rope(q, sq, cq)
            k = _rope(k, sk, ck)
            sim = jnp.einsum('bhnd,bhmd->bhnm', q, k) * DH ** (-0.5)
            a = jax.nn.softmax(sim, axis=-1)
            o = jnp.einsum('bhnm,bhmd->bhnd', a, v)
            o = o.transpose(0, 2, 1, 3).reshape(xq.shape[0], xq.shape[1], MID)
            return o @ wo + bo

        def _adaln(x, c, lw, lb, gw, gb, bw, bb):
            g = (c @ gw + gb)[:, None, :]
            bt = (c @ bw + bb)[:, None, :]
            return _ln(x, lw, lb) * (1.0 + g) + bt
        ks = jax.random.split(jax.random.key(seed), 24)
        s = 0.02
        inp = {'x': jax.random.normal(ks[0], (B, N, D), jnp.float32), 'cond': jax.random.normal(ks[1], (B, D), jnp.float32), 'context': jax.random.normal(ks[2], (B, M, DC), jnp.float32), 'ln1_w': jnp.ones((D,), jnp.float32), 'ln1_b': jnp.zeros((D,), jnp.float32), 'g1_w': jax.random.normal(ks[3], (D, D), jnp.float32) * s, 'g1_b': jnp.zeros((D,), jnp.float32), 'b1_w': jax.random.normal(ks[4], (D, D), jnp.float32) * s, 'b1_b': jnp.zeros((D,), jnp.float32), 'ln2_w': jnp.ones((D,), jnp.float32), 'ln2_b': jnp.zeros((D,), jnp.float32), 'g2_w': jax.random.normal(ks[5], (D, D), jnp.float32) * s, 'g2_b': jnp.zeros((D,), jnp.float32), 'b2_w': jax.random.normal(ks[6], (D, D), jnp.float32) * s, 'b2_b': jnp.zeros((D,), jnp.float32), 'sa_wq': jax.random.normal(ks[7], (D, MID), jnp.float32) * s, 'sa_wkv': jax.random.normal(ks[8], (D, 2 * MID), jnp.float32) * s, 'sa_wo': jax.random.normal(ks[9], (MID, D), jnp.float32) * s, 'sa_bo': jnp.zeros((D,), jnp.float32), 'ca_lnc_w': jnp.ones((DC,), jnp.float32), 'ca_lnc_b': jnp.zeros((DC,), jnp.float32), 'ca_wq': jax.random.normal(ks[10], (D, MID), jnp.float32) * s, 'ca_wkv': jax.random.normal(ks[11], (DC, 2 * MID), jnp.float32) * s, 'ca_wo': jax.random.normal(ks[12], (MID, D), jnp.float32) * s, 'ca_bo': jnp.zeros((D,), jnp.float32), 'ff_w1': jax.random.normal(ks[13], (D, MULT * D), jnp.float32) * s, 'ff_b1': jnp.zeros((MULT * D,), jnp.float32), 'ff_w2': jax.random.normal(ks[14], (MULT * D, D), jnp.float32) * s, 'ff_b2': jnp.zeros((D,), jnp.float32)}
        return inp
    _L1_xcond_all = _L1_xcond_setup()
    _L1_xcond_in = {k: v for k, v in _L1_xcond_all.items() if k in ('ln1_w', 'ln1_b', 'g1_w', 'g1_b', 'b1_w', 'b1_b', 'ln2_w', 'ln2_b', 'g2_w', 'g2_b', 'b2_w', 'b2_b', 'sa_wq', 'sa_wkv', 'sa_wo', 'sa_bo', 'ca_lnc_w', 'ca_lnc_b', 'ca_wq', 'ca_wkv', 'ca_wo', 'ca_bo', 'ff_w1', 'ff_b1', 'ff_w2', 'ff_b2')}
    del _L1_xcond_all
    return {'x': x, 'cond_1024': cond_1024, 'ctx_768': ctx_768, 'L0_xcond_W_ada': _L0_xcond_in['W_ada'], 'L0_xcond_b_ada': _L0_xcond_in['b_ada'], 'L0_xcond_W_qkv': _L0_xcond_in['W_qkv'], 'L0_xcond_b_qkv': _L0_xcond_in['b_qkv'], 'L0_xcond_W_proj': _L0_xcond_in['W_proj'], 'L0_xcond_b_proj': _L0_xcond_in['b_proj'], 'L0_xcond_W_ctx': _L0_xcond_in['W_ctx'], 'L0_xcond_b_ctx': _L0_xcond_in['b_ctx'], 'L0_xcond_W_q': _L0_xcond_in['W_q'], 'L0_xcond_W_k': _L0_xcond_in['W_k'], 'L0_xcond_W_v': _L0_xcond_in['W_v'], 'L0_xcond_W_out': _L0_xcond_in['W_out'], 'L0_xcond_b_out': _L0_xcond_in['b_out'], 'L0_xcond_W_fc1': _L0_xcond_in['W_fc1'], 'L0_xcond_b_fc1': _L0_xcond_in['b_fc1'], 'L0_xcond_W_fc2': _L0_xcond_in['W_fc2'], 'L0_xcond_b_fc2': _L0_xcond_in['b_fc2'], 'L1_xcond_ln1_w': _L1_xcond_in['ln1_w'], 'L1_xcond_ln1_b': _L1_xcond_in['ln1_b'], 'L1_xcond_g1_w': _L1_xcond_in['g1_w'], 'L1_xcond_g1_b': _L1_xcond_in['g1_b'], 'L1_xcond_b1_w': _L1_xcond_in['b1_w'], 'L1_xcond_b1_b': _L1_xcond_in['b1_b'], 'L1_xcond_ln2_w': _L1_xcond_in['ln2_w'], 'L1_xcond_ln2_b': _L1_xcond_in['ln2_b'], 'L1_xcond_g2_w': _L1_xcond_in['g2_w'], 'L1_xcond_g2_b': _L1_xcond_in['g2_b'], 'L1_xcond_b2_w': _L1_xcond_in['b2_w'], 'L1_xcond_b2_b': _L1_xcond_in['b2_b'], 'L1_xcond_sa_wq': _L1_xcond_in['sa_wq'], 'L1_xcond_sa_wkv': _L1_xcond_in['sa_wkv'], 'L1_xcond_sa_wo': _L1_xcond_in['sa_wo'], 'L1_xcond_sa_bo': _L1_xcond_in['sa_bo'], 'L1_xcond_ca_lnc_w': _L1_xcond_in['ca_lnc_w'], 'L1_xcond_ca_lnc_b': _L1_xcond_in['ca_lnc_b'], 'L1_xcond_ca_wq': _L1_xcond_in['ca_wq'], 'L1_xcond_ca_wkv': _L1_xcond_in['ca_wkv'], 'L1_xcond_ca_wo': _L1_xcond_in['ca_wo'], 'L1_xcond_ca_bo': _L1_xcond_in['ca_bo'], 'L1_xcond_ff_w1': _L1_xcond_in['ff_w1'], 'L1_xcond_ff_b1': _L1_xcond_in['ff_b1'], 'L1_xcond_ff_w2': _L1_xcond_in['ff_w2'], 'L1_xcond_ff_b2': _L1_xcond_in['ff_b2']}

def reference(x, cond_1024, ctx_768, L0_xcond_W_ada, L0_xcond_b_ada, L0_xcond_W_qkv, L0_xcond_b_qkv, L0_xcond_W_proj, L0_xcond_b_proj, L0_xcond_W_ctx, L0_xcond_b_ctx, L0_xcond_W_q, L0_xcond_W_k, L0_xcond_W_v, L0_xcond_W_out, L0_xcond_b_out, L0_xcond_W_fc1, L0_xcond_b_fc1, L0_xcond_W_fc2, L0_xcond_b_fc2, L1_xcond_ln1_w, L1_xcond_ln1_b, L1_xcond_g1_w, L1_xcond_g1_b, L1_xcond_b1_w, L1_xcond_b1_b, L1_xcond_ln2_w, L1_xcond_ln2_b, L1_xcond_g2_w, L1_xcond_g2_b, L1_xcond_b2_w, L1_xcond_b2_b, L1_xcond_sa_wq, L1_xcond_sa_wkv, L1_xcond_sa_wo, L1_xcond_sa_bo, L1_xcond_ca_lnc_w, L1_xcond_ca_lnc_b, L1_xcond_ca_wq, L1_xcond_ca_wkv, L1_xcond_ca_wo, L1_xcond_ca_bo, L1_xcond_ff_w1, L1_xcond_ff_b1, L1_xcond_ff_w2, L1_xcond_ff_b2):
    import jax
    import jax.numpy as jnp

    def _L0_xcond_ref(x, c, text_embed, W_ada, b_ada, W_qkv, b_qkv, W_proj, b_proj, W_ctx, b_ctx, W_q, W_k, W_v, W_out, b_out, W_fc1, b_fc1, W_fc2, b_fc2):
        import jax, jax.numpy as jnp
        import numpy as np
        B, N, D, H, TD, TL = (4, 256, 256, 16, 192, 77)
        HD = D // H
        EPS = 1e-06

        def _ln(x):
            mu = jnp.mean(x, axis=-1, keepdims=True)
            var = jnp.var(x, axis=-1, keepdims=True)
            return (x - mu) * jax.lax.rsqrt(var + EPS)

        def _modulate(x, shift, scale):
            return x * (1.0 + scale[:, None, :]) + shift[:, None, :]

        def _heads(t):
            return t.reshape(t.shape[0], t.shape[1], H, HD).transpose(0, 2, 1, 3)

        def _attend(q, k, v):
            sim = jnp.einsum('bhid,bhjd->bhij', q, k) * HD ** (-0.5)
            attn = jax.nn.softmax(sim, axis=-1)
            out = jnp.einsum('bhij,bhjd->bhid', attn, v)
            return out.transpose(0, 2, 1, 3).reshape(out.shape[0], -1, D)
        mod = jax.nn.silu(c) @ W_ada + b_ada
        sh_msa, sc_msa, sh_x, sc_x, sh_mlp, sc_mlp = jnp.split(mod, 6, axis=-1)
        h1 = _modulate(_ln(x), sh_msa, sc_msa)
        qkv = h1 @ W_qkv + b_qkv
        q, k, v = jnp.split(qkv, 3, axis=-1)
        out = _attend(_heads(q), _heads(k), _heads(v))
        x = x + (out @ W_proj + b_proj)
        h2 = _modulate(_ln(x), sh_x, sc_x)
        ctx = text_embed @ W_ctx + b_ctx
        q = _heads(h2 @ W_q)
        k = _heads(ctx @ W_k)
        v = _heads(ctx @ W_v)
        out = _attend(q, k, v)
        x = x + (out @ W_out + b_out)
        h3 = _modulate(_ln(x), sh_mlp, sc_mlp)
        hidden = jax.nn.gelu(h3 @ W_fc1 + b_fc1, approximate=True)
        x = x + (hidden @ W_fc2 + b_fc2)
        return x

    def _L1_xcond_ref(x, cond, context, ln1_w, ln1_b, g1_w, g1_b, b1_w, b1_b, ln2_w, ln2_b, g2_w, g2_b, b2_w, b2_b, sa_wq, sa_wkv, sa_wo, sa_bo, ca_lnc_w, ca_lnc_b, ca_wq, ca_wkv, ca_wo, ca_bo, ff_w1, ff_b1, ff_w2, ff_b2):
        import jax, jax.numpy as jnp
        import numpy as np
        B, N, M = (2, 256, 128)
        D, H, DH = (256, 16, 64)
        MID = H * DH
        DC = 192
        MULT = 4
        EPS = 1e-05

        def _ln(x, w, b):
            mu = jnp.mean(x, -1, keepdims=True)
            var = jnp.mean((x - mu) ** 2, -1, keepdims=True)
            return (x - mu) * jax.lax.rsqrt(var + EPS) * w + b

        def _sincos(n, d):
            inv = 1.0 / 10000.0 ** (jnp.arange(0, d, 2, dtype=jnp.float32) / d)
            ang = jnp.arange(n, dtype=jnp.float32)[:, None] * inv[None, :]
            return (jnp.sin(ang), jnp.cos(ang))

        def _rope(x, sin, cos):
            s = sin[None, None]
            c = cos[None, None]
            xe = x[..., ::2]
            xo = x[..., 1::2]
            re = xe * c - xo * s
            ro = xe * s + xo * c
            return jnp.stack((re, ro), axis=-1).reshape(x.shape)

        def _heads(t):
            b, n, _ = t.shape
            return t.reshape(b, n, H, DH).transpose(0, 2, 1, 3)

        def _attn(xq, ctx, wq, wkv, wo, bo):
            q = _heads(xq @ wq)
            k, v = jnp.split(ctx @ wkv, 2, axis=-1)
            k = _heads(k)
            v = _heads(v)
            sq, cq = _sincos(q.shape[2], DH)
            sk, ck = _sincos(k.shape[2], DH)
            q = _rope(q, sq, cq)
            k = _rope(k, sk, ck)
            sim = jnp.einsum('bhnd,bhmd->bhnm', q, k) * DH ** (-0.5)
            a = jax.nn.softmax(sim, axis=-1)
            o = jnp.einsum('bhnm,bhmd->bhnd', a, v)
            o = o.transpose(0, 2, 1, 3).reshape(xq.shape[0], xq.shape[1], MID)
            return o @ wo + bo

        def _adaln(x, c, lw, lb, gw, gb, bw, bb):
            g = (c @ gw + gb)[:, None, :]
            bt = (c @ bw + bb)[:, None, :]
            return _ln(x, lw, lb) * (1.0 + g) + bt
        attn_in = _adaln(x, cond, ln1_w, ln1_b, g1_w, g1_b, b1_w, b1_b)
        x = _attn(attn_in, attn_in, sa_wq, sa_wkv, sa_wo, sa_bo) + x
        cross_in = _adaln(x, cond, ln1_w, ln1_b, g1_w, g1_b, b1_w, b1_b)
        ctx_n = _ln(context, ca_lnc_w, ca_lnc_b)
        x = _attn(cross_in, ctx_n, ca_wq, ca_wkv, ca_wo, ca_bo) + x
        ffn_in = _adaln(x, cond, ln2_w, ln2_b, g2_w, g2_b, b2_w, b2_b)
        h = jax.nn.gelu(ffn_in @ ff_w1 + ff_b1, approximate=False)
        x = h @ ff_w2 + ff_b2 + x
        return x
    x = _L0_xcond_ref(x, cond_1024, ctx_768, L0_xcond_W_ada, L0_xcond_b_ada, L0_xcond_W_qkv, L0_xcond_b_qkv, L0_xcond_W_proj, L0_xcond_b_proj, L0_xcond_W_ctx, L0_xcond_b_ctx, L0_xcond_W_q, L0_xcond_W_k, L0_xcond_W_v, L0_xcond_W_out, L0_xcond_b_out, L0_xcond_W_fc1, L0_xcond_b_fc1, L0_xcond_W_fc2, L0_xcond_b_fc2)
    x = _L1_xcond_ref(x, cond_1024, ctx_768, L1_xcond_ln1_w, L1_xcond_ln1_b, L1_xcond_g1_w, L1_xcond_g1_b, L1_xcond_b1_w, L1_xcond_b1_b, L1_xcond_ln2_w, L1_xcond_ln2_b, L1_xcond_g2_w, L1_xcond_g2_b, L1_xcond_b2_w, L1_xcond_b2_b, L1_xcond_sa_wq, L1_xcond_sa_wkv, L1_xcond_sa_wo, L1_xcond_sa_bo, L1_xcond_ca_lnc_w, L1_xcond_ca_lnc_b, L1_xcond_ca_wq, L1_xcond_ca_wkv, L1_xcond_ca_wo, L1_xcond_ca_bo, L1_xcond_ff_w1, L1_xcond_ff_b1, L1_xcond_ff_w2, L1_xcond_ff_b2)
    return x

_drawn_inputs = setup_inputs


def setup_inputs(seed=0):
    import zlib

    import numpy as np

    out = dict(_drawn_inputs(seed))
    spreads = {'L0_xcond_b_ada': (0.0, 0.393),
     'L0_xcond_b_qkv': (0.0, 0.1),
     'L0_xcond_b_proj': (0.0, 0.1),
     'L0_xcond_b_ctx': (0.0, 0.78),
     'L0_xcond_b_out': (0.0, 0.1),
     'L0_xcond_b_fc1': (0.0, 0.397),
     'L0_xcond_b_fc2': (0.0, 0.1),
     'L1_xcond_ln1_w': (1.0, 0.6),
     'L1_xcond_ln1_b': (0.0, 0.389),
     'L1_xcond_g1_b': (0.0, 0.8),
     'L1_xcond_b1_b': (0.0, 0.427),
     'L1_xcond_ln2_w': (1.0, 0.6),
     'L1_xcond_ln2_b': (0.0, 0.741),
     'L1_xcond_g2_b': (0.0, 0.793),
     'L1_xcond_b2_b': (0.0, 0.731),
     'L1_xcond_sa_bo': (0.0, 0.1),
     'L1_xcond_ca_lnc_w': (1.0, 0.6),
     'L1_xcond_ca_lnc_b': (0.0, 0.487),
     'L1_xcond_ca_bo': (0.0, 0.1),
     'L1_xcond_ff_b1': (0.0, 0.375),
     'L1_xcond_ff_b2': (0.0, 0.1)}
    factors = {'L0_xcond_W_ctx': 4.027,
     'L0_xcond_W_q': 8.0,
     'L0_xcond_W_k': 8.0,
     'L0_xcond_W_v': 3.206,
     'L0_xcond_W_out': 3.225,
     'L1_xcond_g1_w': 3.993,
     'L1_xcond_sa_wq': 8.0,
     'L1_xcond_ca_wq': 8.0,
     'L1_xcond_b2_w': 2.68}
    for name, (base, spread) in spreads.items():
        noise = np.random.default_rng([zlib.crc32(name.encode()), seed]).standard_normal(out[name].shape)
        drawn = base * np.exp(spread * noise) if base else spread * noise
        out[name] = jnp.asarray(drawn.astype(out[name].dtype))
    for name, factor in factors.items():
        out[name] = (out[name] * factor).astype(out[name].dtype)
    return out
```

```python
from contextlib import ExitStack

import numpy as np

import concourse.bass as bass
from concourse import mybir

F32 = mybir.dt.float32
ALU = mybir.AluOpType
ACT = mybir.ActivationFunctionType
AX_X = mybir.AxisListType.X

P = 128
B, N, D = 32, 100, 256
M, DC = 361, 192
H = 16
FF = 4 * D
PAIR = 2
ROUNDS = B // PAIR
T = PAIR * N
C = D // P
CF = FF // P
KC = 96
CC = DC // KC
MP = 121
MCH = [(m, min(MP, M - m)) for m in range(0, M, MP)]
NM = len(MCH)
HD = [D // H, 64]
WIDTH = [H * d for d in HD]
CW = [w // P for w in WIDTH]
EPS = [1e-6, 1e-5]
SCALE = [d ** -0.5 for d in HD]
SELF_HEADS = 4
BANK = 512
HEADS_OF = {"self": SELF_HEADS, "cross": 1}
KEYS_OF = {"self": N, "cross": M}
GROUPS_OF = {k: PAIR * H // n for k, n in HEADS_OF.items()}
GROUPS = sum(GROUPS_OF.values())
TOK_PARTS = [1, 2]
TOK_JOBS = [PAIR * (2 * parts + 3) for parts in TOK_PARTS]
NORMS = [3, 4]
ROT = 4
ROTATIONS = 3 * CW[1] // ROT + PAIR * CW[1] // 2
SWAP = [(p + 16) % 32 for p in range(32)]
VECTOR_MARKS = [3 * 4 + 2 * PAIR * TOK_PARTS[0],
                3 * 4 + 3 * PAIR * NM + 2 * PAIR * TOK_PARTS[1] + 3 * ROTATIONS]

COLS = [("b_ada", 12), ("b_qkv", 6), ("b_ctx", 2), ("b_fc1_0", 8), ("b_fc1_1", 8), ("ln_w", 4), ("ln_b", 4),
        ("g_b", 4), ("beta_b", 4), ("lnc_w", 2), ("lnc_b", 2), ("mask", 8)]
ROWS = 6


def lin_order(L):
    cw, banks = CW[L], TOK_PARTS[L]
    ctx_k = [("ctx_k", PAIR * cw)]
    ctx_t = [("ctx_t", PAIR * CC)]
    sorts = (ctx_k if L == 0 else []) + [("t0", C), ("q", cw), ("k", cw), ("v", PAIR * banks)]
    sorts += (ctx_t + ctx_k if L == 1 else []) + [("ctx_v0", NM * banks), ("ctx_v1", NM * banks)]
    sorts += [("o1", PAIR * banks), ("t1", C), ("q2", cw), ("o2", PAIR * banks), ("t2", C), ("f1", CF)]
    first, n = {}, 0
    for name, count in sorts:
        first[name] = n
        n += count
    assert n % 2 == 0
    return first, n


class Count:

    def __init__(self, i, per, start=0):
        self.i, self.per, self.start, self.n = i, per, start, 0

    def at(self, n):
        return self.i * self.per + (self.start + n)

    def next(self):
        self.n += 1
        return self.at(self.n)

    def end(self):
        assert self.n == self.per, (self.n, self.per)


def group_heads(kind, g):
    if kind == "cross":
        return g // H, [g % H]
    b, q = divmod(g, H // SELF_HEADS)
    first = q // 2 * 2 * SELF_HEADS + q % 2
    return b, list(range(first, first + 2 * SELF_HEADS, 2))


def spread(ap, shape):
    return ap.rearrange("p (m o) -> p m o", o=1).broadcast_to(shape)


def two_blocks(nc, a, out):
    with ExitStack() as ctx:
        def sb(name, shape):
            return ctx.enter_context(nc.sbuf_tensor(name, list(shape), F32))

        def sem(name):
            return ctx.enter_context(nc.semaphore(name))

        lin, sc, tr, tok = (ctx.enter_context(nc.psum_tensor(n, [P, 2, BANK], F32)) for n in ("lin", "sc", "tr", "tok"))

        w1 = {n: sb("w1_" + n, a["w1_" + n].shape) for n in ("q", "k", "v", "o", "cq", "ck", "cv", "co", "f1", "f2")}
        cols = sb("cols_sb", [P, sum(n for _, n in COLS)])
        ident, rows = sb("ident_sb", [P, P]), sb("rows_sb", [N, ROWS, D])
        cos, sin = sb("cos_sb", [P, M]), sb("sin_sb", [P, M])
        mods = [sb("mod0", [P, 12, B]), sb("mod1", [P, 8, B])]
        modcur = sb("modcur", [P, 12, PAIR])
        derived = sb("derived", [P, 3, C])
        half = sb("half", [P, 2 * NM])
        norm = {n: sb(n, s) for n, s in (("stats", [P, 6, 6]), ("mv", [P, 6, 2]), ("veps", [P, 6]), ("rstd", [P, 6]))}
        soft = {n: sb(n, [N, PAIR, H]) for n in ("negmax", "sums", "rinv")}
        arena = sb("arena", [P, ARENA])
        used = [0]

        def carve(p, *shape):
            n = int(np.prod(shape))
            ap = arena[0:p, used[0]:used[0] + n]
            used[0] += n
            assert used[0] <= ARENA, used[0]
            dims = "abcd"[:len(shape)]
            if len(shape) > 1:
                ap = ap.rearrange(f"p ({' '.join(dims)}) -> p {' '.join(dims)}", **dict(zip(dims, shape)))
            return ap

        at, pos = {}, 0
        for name, n in COLS:
            at[name] = cols[:, pos:pos + n]
            pos += n
        at["bq"], at["b_ck"], at["b_cv"] = derived[:, 0], derived[:, 1], derived[:, 2]

        x_mid = nc.dram_tensor("x_mid", [B, N, D], F32, kind="Internal").ap()
        w1_loaded = sem("w1_loaded")

        w0 = {n: carve(P, *a["w0_" + n].shape[1:]) for n in ("qkv", "o", "cq", "co", "f1", "f2")}
        w0["ck"], w0["cv"] = carve(KC, CC, D), carve(KC, CC, D)
        layer0_start = used[0]
        setup(nc, sem, carve, a, at, w0, w1, cols, ident, rows, cos, sin, mods, derived, half, lin, sc, tr, w1_loaded)
        used[0] = layer0_start
        layer(nc, 0, sem, carve, a, at, w0, a["x"], x_mid, ident, rows, mods[0], modcur, half, norm, soft,
              lin, sc, tr, tok, cos, sin, w1_loaded)
        used[0] = 0
        layer(nc, 1, sem, carve, a, at, w1, x_mid, out, ident, rows, mods[1], modcur, half, norm, soft,
              lin, sc, tr, tok, cos, sin, w1_loaded)


ARENA = 28900


def setup(nc, sem, carve, a, at, w0, w1, cols, ident, rows, cos, sin, mods, derived, half, lin, sc, tr, w1_loaded):
    wada, wmod = carve(P, C, 12 * P), carve(P, 4, C, D)
    wctxT, wk, wv = carve(P, C, DC), carve(P, C, D), carve(P, C, D)
    condT, silu_c, gain = carve(P, C, B), carve(P, C, B), carve(P, 2, C, B)
    vectors_loaded, factors_loaded, rest_loaded = sem("vectors_loaded"), sem("factors_loaded"), sem("rest_loaded")
    silu_done, folded_out = sem("silu_done"), sem("folded_out")
    mod0_ready, mod1_ready, fold_ready, bias_ready = (sem(n) for n in ("mod0_ready", "mod1_ready", "fold_ready", "bias_ready"))
    step = sem("setup_step")

    with nc.Block() as block:
        @block.sync
        def _(sp):
            sp.dma_start(condT, a["condT"]).then_inc(vectors_loaded, 16)
            sp.dma_start(cols[:], a["cols"]).then_inc(vectors_loaded, 16)
            for dst, name in ((wada, "wada"), (wmod, "wmod"), (wctxT, "wctxT"), (wk, "w0_k"), (wv, "w0_v")):
                sp.dma_start(dst, a[name]).then_inc(factors_loaded, 16)
            loads = [(w0[n], a["w0_" + n]) for n in ("qkv", "o", "cq", "co", "f1", "f2")]
            loads += [(ident[:], a["ident"]), (cos[:], a["cos"]), (sin[:], a["sin"]),
                      (rows[:], a["rows"].partition_broadcast(N))]
            for dst, src in loads:
                sp.dma_start(dst, src).then_inc(rest_loaded, 16)
            for name, dst in w1.items():
                sp.dma_start(dst[:], a["w1_" + name]).then_inc(w1_loaded, 16)
            sp.wait_ge(rest_loaded, 16 * len(loads))

        @block.scalar
        def _(act):
            act.wait_ge(vectors_loaded, 32)
            nc.scalar.activation(silu_c, condT, ACT.Silu).then_inc(silu_done, 1)
            act.wait_ge(fold_ready, 1)
            for bank, dst in enumerate((w0["ck"], w0["cv"])):
                nc.scalar.copy(dst, sc[0:KC, bank, 0:CC * D].rearrange("p (c n) -> p c n", c=CC)).then_inc(folded_out, 1)
            act.wait_ge(folded_out, 2)

        @block.tensor
        def _(pe):
            pe.wait_ge(silu_done, 1)
            pe.wait_ge(factors_loaded, 80)
            for m in range(12):
                for c in range(C):
                    mm = nc.tensor.matmul(lin[:, 0, m * B:(m + 1) * B], wada[:, c, m * P:(m + 1) * P],
                                          silu_c[:, c, :], start=(c == 0), stop=(c == C - 1))
            mm.then_inc(mod0_ready, 1)
            for k in range(4):
                for m in range(C):
                    o = (k * C + m) * B
                    for c in range(C):
                        mm = nc.tensor.matmul(lin[:, 1, o:o + B], wmod[:, k, c, m * P:(m + 1) * P],
                                              condT[:, c, :], start=(c == 0), stop=(c == C - 1))
            mm.then_inc(mod1_ready, 1)
            for bank, w in enumerate((wk, wv)):
                for r in range(CC):
                    for c in range(C):
                        mm = nc.tensor.matmul(sc[0:KC, bank, r * D:(r + 1) * D], wctxT[:, c, r * KC:(r + 1) * KC],
                                              w[:, c, :], start=(c == 0), stop=(c == C - 1))
            mm.then_inc(fold_ready, 1)
            for j, w in enumerate((wk, wv)):
                for m in range(C):
                    for c in range(C):
                        mm = nc.tensor.matmul(tr[:, 0, C * j + m:C * j + m + 1], w[:, c, m * P:(m + 1) * P],
                                              at["b_ctx"][:, c:c + 1], start=(c == 0), stop=(c == C - 1))
            mm.then_inc(bias_ready, 1)

        @block.vector
        def _(dve):
            done = [0]

            def then_wait(ins):
                done[0] += 1
                ins.then_inc(step, 1)
                dve.wait_ge(step, done[0])

            then_wait(nc.vector.memset(half[:], -0.5))
            dve.wait_ge(vectors_loaded, 32)
            then_wait(nc.vector.tensor_scalar(derived[:, 0], at["b_qkv"][:, 0:C], SCALE[0], None, ALU.mult))
            dve.wait_ge(mod0_ready, 1)
            then_wait(nc.vector.tensor_tensor(mods[0][:], lin[:, 0, 0:12 * B].rearrange("p (m b) -> p m b", b=B),
                                              spread(at["b_ada"], [P, 12, B]), ALU.add))
            for s in range(3):
                scale = mods[0][:, 4 * s + C:4 * s + 2 * C, :]
                then_wait(nc.vector.tensor_scalar(scale, scale, 1.0, None, ALU.add))
            dve.wait_ge(mod1_ready, 1)
            for k in range(2):
                g, beta = (lin[:, 1, j * C * B:(j + 1) * C * B].rearrange("p (m b) -> p m b", b=B) for j in (2 * k, 2 * k + 1))
                of = {n: spread(at[n][:, k * C:(k + 1) * C], [P, C, B]) for n in ("g_b", "ln_w", "ln_b", "beta_b")}
                shift, scale = mods[1][:, 4 * k:4 * k + C, :], mods[1][:, 4 * k + C:4 * k + 2 * C, :]
                then_wait(nc.vector.tensor_tensor(gain[:, 0], g, of["g_b"], ALU.add))
                then_wait(nc.vector.tensor_scalar(gain[:, 0], gain[:, 0], 1.0, None, ALU.add))
                then_wait(nc.vector.tensor_tensor(scale, gain[:, 0], of["ln_w"], ALU.mult))
                then_wait(nc.vector.tensor_tensor(gain[:, 1], gain[:, 0], of["ln_b"], ALU.mult))
                then_wait(nc.vector.tensor_tensor(shift, beta, gain[:, 1], ALU.add))
                then_wait(nc.vector.tensor_tensor(shift, shift, of["beta_b"], ALU.add))
            dve.wait_ge(bias_ready, 1)
            then_wait(nc.vector.tensor_copy(derived[:, 1:3], tr[:, 0, 0:2 * C].rearrange("p (j c) -> p j c", c=C)))


def layer(nc, L, sem_of, carve, a, at, w, x_src, x_dst, ident, rows, mod, modcur, half, norm, soft,
          lin, sc, tr, tok, cos, sin, w1_loaded):
    hd, cw, width, parts = HD[L], CW[L], WIDTH[L], TOK_PARTS[L]
    stats, mv, veps, rstd = (norm[n] for n in ("stats", "mv", "veps", "rstd"))
    negmax, sums, rinv = (soft[n] for n in ("negmax", "sums", "rinv"))
    J, LIN = lin_order(L)
    TOK = TOK_JOBS[L]
    QS = cw if L == 0 else cw // ROT
    QREADY = 2 * cw if L == 0 else ROTATIONS
    part_heads = H // parts
    part_cols = width // parts
    part_chunks = cw // parts
    w_q = w["qkv"][:, :, 0:D] if L == 0 else w["q"]
    w_k = w["qkv"][:, :, D:2 * D] if L == 0 else w["k"]
    w_v = w["qkv"][:, :, 2 * D:3 * D] if L == 0 else w["v"]
    row = 3 * L

    def sem(name):
        return sem_of(f"{name}_{L}")

    x_in = carve(N, PAIR, D)
    x_now = carve(N, PAIR, D)
    x_bias = carve(N, PAIR, D)
    xn = carve(N, PAIR, D)
    hT = carve(P, C, T)
    qT, kT = carve(P, cw, T), carve(P, cw, T)
    v_self = carve(N, PAIR, width)
    kc = carve(P, PAIR, cw, M)
    vc = carve(MP, PAIR, NM, width)
    ctxT = carve(KC, PAIR, CC, M)
    prob = carve(N, 2, 400)
    probT = carve(MP, 2, 400)
    o_tok = carve(N, PAIR, width)
    oT = carve(P, cw, T)
    if L == 0:
        qmask = carve(P, cw, P // hd, T)
        gT = carve(P, CF, T)
    else:
        gT = qT
        ctx_in = carve(MP, PAIR * NM, DC)
        swapped = carve(P, ROT * T)

    x_loaded, ctx_loaded, x_stored = sem("x_loaded"), sem("ctx_loaded"), sem("x_stored")
    x_in_free, ctx_free = sem("x_in_free"), sem("ctx_free")
    lin_ready, lin_out = sem("lin_ready"), sem("lin_out")
    tok_ready, tok_out = sem("tok_ready"), sem("tok_out")
    sc_ready, max_ready, prob_ready = sem("sc_ready"), sem("max_ready"), sem("prob_ready")
    tr_ready, probT_ready = sem("tr_ready"), sem("probT_ready")
    var_ready, rstd_ready, xn_ready = sem("var_ready"), sem("rstd_ready"), sem("xn_ready")
    bias_added, mod_ready = sem("bias_added"), sem("mod_ready")
    q_ready = sem("q_ready")
    cleared, step, stats_seen = sem("cleared"), sem("vector_step"), sem("stats_seen")
    ctx_dmas = PAIR if L == 0 else 2 * PAIR

    with nc.Block() as block:
        @block.sync
        def _(sp):
            sp.sem_inc(x_stored, 16)
            if L == 1:
                sp.wait_ge(w1_loaded, 16 * len(w))
                sp.wait_ge(cleared, 1)
            with nc.Fori(0, ROUNDS, engines=[sp.engine]) as i:
                sp.wait_ge(ctx_free, i + 1)
                for b in range(PAIR):
                    if L == 0:
                        sp.dma_start(ctxT[:, b], a["ctxT"][bass.ds(i * PAIR + b, 1)].rearrange("o p c m -> (o p) c m"))\
                          .then_inc(ctx_loaded, 16)
                    else:
                        src = a["ctx"][bass.ds(i * PAIR + b, 1)].rearrange("o m d -> (o m) d")
                        whole, rest = MCH[-1]
                        sp.dma_start(ctx_in[:, b * NM:b * NM + NM - 1, :],
                                     src[0:whole].rearrange("(t p) d -> p t d", p=MP)).then_inc(ctx_loaded, 16)
                        sp.dma_start(ctx_in[0:rest, b * NM + NM - 1, :], src[whole:M]).then_inc(ctx_loaded, 16)
                sp.wait_ge(x_in_free, i + 1)
                sp.dma_start(x_in, x_src[bass.ds(i * PAIR, PAIR)].rearrange("b n d -> n b d")).then_inc(x_loaded, 16)
                sp.wait_ge(tok_out, i * TOK + (2 + TOK))
                sp.dma_start(x_dst[bass.ds(i * PAIR, PAIR)].rearrange("b n d -> n b d"), x_now).then_inc(x_stored, 16)
            sp.wait_ge(x_stored, 16 * (ROUNDS + 1))

        @block.gpsimd
        def _(pool):
            pool.sem_inc(x_in_free, 1)
            pool.sem_inc(ctx_free, 1)
            with nc.Fori(0, ROUNDS, engines=[pool.engine]) as i:
                roots = Count(i, NORMS[L])
                pool.wait_ge(lin_out, i * LIN + 2)
                n_mod = mod.shape[1]
                nc.gpsimd.tensor_copy(modcur[:, 0:n_mod, :], mod[:, :, bass.ds(i * PAIR, PAIR)]).then_inc(mod_ready, 1)

                def inverse_root(p, n):
                    pool.wait_ge(var_ready, roots.next())
                    nc.gpsimd.tensor_tensor(rstd[0:p, 0:n], veps[0:p, 0:n], half[0:p, 0:n], ALU.pow).then_inc(rstd_ready, 1)

                def add_bias(src, r):
                    nc.gpsimd.tensor_tensor(x_bias, src, rows[:, r:r + 1, :].broadcast_to([N, PAIR, D]), ALU.add)\
                      .then_inc(bias_added, 1)

                inverse_root(N, PAIR)
                pool.wait_ge(tok_out, i * TOK + 2)
                pool.wait_ge(x_loaded, i * 16 + 16)
                add_bias(x_in, row)
                pool.wait_ge(xn_ready, i * 6 + 2)
                pool.wait_ge(bias_added, i * 3 + 1)
                pool.sem_inc(x_in_free, 1)
                if L == 1:
                    inverse_root(MP, PAIR * NM)
                for stage in (1, 2):
                    inverse_root(N, PAIR)
                    add_bias(x_now, row + stage)
                roots.end()

        @block.scalar
        def _(act):
            act.sem_inc(lin_out, 2)
            with nc.Fori(0, ROUNDS, engines=[act.engine]) as i:
                filled = Count(i, LIN)
                maxima = Count(i, GROUPS)

                def filled_bank():
                    n = filled.n
                    act.wait_ge(lin_ready, filled.next())
                    return lin[:, n % 2]

                def evict_modulated(stage):
                    s = 2 * C * (stage if L == 0 else stage // 2)
                    for c in range(C):
                        ps = filled_bank()
                        if stage == 0 and c == 0:
                            act.wait_ge(mod_ready, i + 1)
                        for b in range(PAIR):
                            ins = nc.scalar.activation(hT[:, c, b * N:(b + 1) * N], ps[:, b * N:(b + 1) * N], ACT.Identity,
                                                       bias=modcur[:, s + c, b:b + 1], scale=modcur[:, s + C + c, b:b + 1])
                        ins.then_inc(lin_out, 1)

                def evict_chunks(dst, n, scale, bias=None):
                    for c in range(cw):
                        ps = filled_bank()
                        if bias is None:
                            nc.scalar.activation(dst[:, c, :], ps[:, 0:n], ACT.Copy, scale=scale).then_inc(lin_out, 1)
                        else:
                            nc.scalar.activation(dst[:, c, :], ps[:, 0:n], ACT.Identity, scale=scale,
                                                 bias=bias[:, c:c + 1]).then_inc(lin_out, 1)

                def evict_context_keys():
                    for b in range(PAIR):
                        evict_chunks(kc[:, b], M, 1.0, at["b_ck"] if L == 0 else None)

                def evict_context_values(b):
                    for t, (_, mn) in enumerate(MCH):
                        for h in range(parts):
                            ps = filled_bank()
                            nc.scalar.copy(vc[0:mn, b, t, h * part_cols:(h + 1) * part_cols], ps[0:mn, 0:part_cols])\
                              .then_inc(lin_out, 1)

                def probabilities(kind):
                    keys = KEYS_OF[kind]
                    for g in range(GROUPS_OF[kind]):
                        n = maxima.n
                        b, hs = group_heads(kind, g)
                        act.wait_ge(max_ready, maxima.next())
                        for k, h in enumerate(hs):
                            ins = nc.scalar.activation(prob[:, n % 2, k * keys:(k + 1) * keys],
                                                       sc[0:N, n % 2, k * keys:(k + 1) * keys], ACT.Exp,
                                                       bias=negmax[:, b, h:h + 1], accum_out=sums[:, b, h:h + 1])
                        ins.then_inc(prob_ready, 1)

                def evict_attention(bias):
                    for b in range(PAIR):
                        for h in range(parts):
                            ps = filled_bank()[:, 0:part_chunks * N].rearrange("p (c n) -> p c n", n=N)
                            dst = oT[:, h * part_chunks:(h + 1) * part_chunks, b * N:(b + 1) * N]
                            if bias is None:
                                ins = nc.scalar.copy(dst, ps)
                            else:
                                for c in range(part_chunks):
                                    ins = nc.scalar.activation(dst[:, c], ps[:, c], ACT.Identity, bias=bias[:, c:c + 1])
                            ins.then_inc(lin_out, 1)

                if L == 0:
                    evict_context_keys()
                evict_modulated(0)
                evict_chunks(qT, T, SCALE[L], at["bq"] if L == 0 else None)
                evict_chunks(kT, T, 1.0, at["b_qkv"][:, C:2 * C] if L == 0 else None)
                for b in range(PAIR):
                    for h in range(parts):
                        ps = filled_bank()
                        nc.scalar.copy(v_self[:, b, h * part_cols:(h + 1) * part_cols], ps[0:N, 0:part_cols])\
                          .then_inc(lin_out, 1)
                if L == 1:
                    for b in range(PAIR):
                        for c in range(CC):
                            ps = filled_bank()
                            nc.scalar.activation(ctxT[:, b, c, :], ps[0:KC, 0:M], ACT.Identity,
                                                 bias=at["lnc_b"][0:KC, c:c + 1],
                                                 scale=at["lnc_w"][0:KC, c:c + 1]).then_inc(lin_out, 1)
                    evict_context_keys()
                evict_context_values(0)
                evict_context_values(1)
                probabilities("self")
                evict_attention(at["b_qkv"][:, 2 * C:3 * C] if L == 0 else None)
                evict_modulated(1)
                evict_chunks(qT, T, SCALE[L])
                probabilities("cross")
                evict_attention(at["b_cv"] if L == 0 else None)
                evict_modulated(2)
                for m in range(CF):
                    ps = filled_bank()
                    nc.scalar.activation(gT[:, m, :], ps[:, 0:T], ACT.Gelu_apprx_tanh if L == 0 else ACT.Gelu,
                                         bias=at[f"b_fc1_{L}"][:, m:m + 1]).then_inc(lin_out, 1)
                filled.end()
                maxima.end()

        @block.vector
        def _(dve):
            if L == 1:
                nc.vector.memset(ctx_in, 0.0)
            nc.vector.memset(tr[:], 0.0).then_inc(cleared, 1)
            dve.sem_inc(tok_out, 2)
            with nc.Fori(0, ROUNDS, engines=[dve.engine]) as i:
                marks = Count(i, VECTOR_MARKS[L])
                toks = Count(i, TOK)
                groups = Count(i, GROUPS)
                roots = Count(i, NORMS[L])
                rows_done = Count(i, 6)
                chunks = Count(i, QREADY)

                def mark(ins):
                    ins.then_inc(step, 1)
                    return marks.next()

                def normalise(src, dst, p, n, done):
                    first = [mark(nc.vector.bn_stats(stats[0:p, s, :], src[:, s])) for s in range(n)]
                    dve.wait_ge(step, first[-1])
                    dve.sem_inc(stats_seen, 1)
                    for s in range(n):
                        last = mark(nc.vector.bn_aggr(mv[0:p, s, :], stats[0:p, s, :]))
                    dve.wait_ge(step, last)
                    nc.vector.tensor_scalar(veps[0:p, 0:n], mv[0:p, 0:n, 1], EPS[L], None, ALU.add).then_inc(var_ready, 1)
                    dve.wait_ge(rstd_ready, roots.next())
                    for s in range(n):
                        done(nc.vector.tensor_scalar(dst[:, s], src[:, s], mv[0:p, s, 0:1], rstd[0:p, s:s + 1],
                                                     ALU.subtract, ALU.mult))

                def normalise_rows(src):
                    def done(ins):
                        ins.then_inc(xn_ready, 1)
                        rows_done.next()

                    normalise(src, xn, N, PAIR, done)

                def mask_queries(name):
                    for c in range(cw):
                        dve.wait_ge(lin_out, i * LIN + (2 + J[name] + c + 1))
                        nc.vector.tensor_tensor(qmask[:, c], qT[:, c:c + 1, :].broadcast_to([P, P // hd, T]),
                                                spread(at["mask"], [P, P // hd, T]), ALU.mult).then_inc(q_ready, 1)
                        chunks.next()

                def rotate(buf, last_job, reps, n):
                    def runs(ap):
                        return ap.rearrange("p (r n) -> p r n", n=n)

                    def table(t):
                        return t[:, 0:n].unsqueeze(1).broadcast_to([P, reps, n])

                    sw = swapped[:, 0:reps * n]
                    dve.wait_ge(lin_out, i * LIN + (2 + last_job + 1))
                    by_sin = mark(nc.vector.tensor_tensor(runs(sw), runs(buf), table(sin), ALU.mult))
                    dve.wait_ge(step, by_sin)
                    mark(nc.vector.tensor_tensor(runs(buf), runs(buf), table(cos), ALU.mult))
                    shuffled = mark(nc.vector.stream_shuffle(sw, sw, SWAP))
                    dve.wait_ge(step, shuffled)
                    nc.vector.tensor_tensor(buf, buf, sw, ALU.add).then_inc(q_ready, 1)
                    dve.wait_ge(q_ready, chunks.next())

                def rotate_tokens(dst, name):
                    for c in range(0, cw, ROT):
                        rotate(dst[:, c:c + ROT, :].rearrange("p c t -> p (c t)"), J[name] + c + ROT - 1, ROT * PAIR, N)

                def attend(kind):
                    heads, keys, total = HEADS_OF[kind], KEYS_OF[kind], GROUPS_OF[kind]
                    g0 = groups.n
                    part_groups = part_heads // heads
                    for s in range(total + 3):
                        if s < total:
                            n = g0 + s
                            b, hs = group_heads(kind, s)
                            dve.wait_ge(sc_ready, groups.next())
                            nc.vector.tensor_reduce(negmax[:, b, hs[0]:hs[-1] + 1:2],
                                                    sc[0:N, n % 2, 0:heads * keys].rearrange("p (h k) -> p h k", h=heads),
                                                    AX_X, ALU.max, negate=True).then_inc(max_ready, 1)
                        if 1 <= s <= total:
                            n = g0 + s - 1
                            p, used = (N, heads * N) if kind == "self" else (MP, NM * N)
                            dve.wait_ge(tr_ready, groups.at(n + 1))
                            nc.vector.tensor_copy(probT[0:p, n % 2, 0:used], tr[0:p, n % 2, 0:used]).then_inc(probT_ready, 1)
                        if s >= 3 and (s - 2) % part_groups == 0:
                            b, part = divmod((s - 2) // part_groups - 1, parts)
                            hs = slice(part * part_heads, (part + 1) * part_heads)
                            bank = toks.n % 2
                            dve.wait_ge(tok_ready, toks.next())
                            inverted = mark(nc.vector.reciprocal(rinv[:, b, hs], sums[:, b, hs]))
                            dve.wait_ge(step, inverted)
                            nc.vector.tensor_tensor(
                                o_tok[:, b, part * part_cols:(part + 1) * part_cols].rearrange("p (h d) -> p h d", d=hd),
                                tok[0:N, bank, 0:part_cols].rearrange("p (h d) -> p h d", d=hd),
                                spread(rinv[:, b, hs], [N, part_heads, hd]), ALU.mult).then_inc(tok_out, 1)

                def add_residual(stage):
                    dve.wait_ge(bias_added, i * 3 + (stage + 1))
                    if stage == 0:
                        dve.wait_ge(x_stored, i * 16 + 16)
                    for b in range(PAIR):
                        bank = toks.n % 2
                        dve.wait_ge(tok_ready, toks.next())
                        nc.vector.tensor_tensor(x_now[:, b], tok[0:N, bank, 0:D], x_bias[:, b], ALU.add).then_inc(tok_out, 1)
                    dve.wait_ge(tok_out, toks.at(toks.n + 2))

                dve.wait_ge(x_loaded, i * 16 + 16)
                normalise_rows(x_in)
                if L == 0:
                    mask_queries("q")
                else:
                    dve.wait_ge(ctx_loaded, i * (16 * ctx_dmas) + 16 * ctx_dmas)
                    normalise(ctx_in, ctx_in, MP, PAIR * NM, mark)
                    rotate_tokens(qT, "q")
                    rotate_tokens(kT, "k")
                    for b in range(PAIR):
                        for c in range(0, cw, 2):
                            rotate(kc[:, b, c:c + 2, :].rearrange("p c t -> p (c t)"), J["ctx_k"] + b * cw + c + 1, 2, M)
                attend("self")
                add_residual(0)
                normalise_rows(x_now)
                if L == 0:
                    mask_queries("q2")
                else:
                    rotate_tokens(qT, "q2")
                attend("cross")
                add_residual(1)
                normalise_rows(x_now)
                add_residual(2)
                for count in (marks, toks, groups, roots, rows_done, chunks):
                    count.end()

        @block.tensor
        def _(pe):
            if L == 1:
                pe.wait_ge(w1_loaded, 16 * len(w))
            pe.wait_ge(cleared, 1)
            with nc.Fori(0, ROUNDS, engines=[pe.engine], hint_back_edge=True) as i:
                jobs = Count(i, LIN)
                toks = Count(i, TOK)
                groups = Count(i, GROUPS)

                def free_lin():
                    n = jobs.n
                    pe.wait_ge(lin_out, jobs.next())
                    return lin[:, n % 2]

                def free_tok():
                    n = toks.n
                    pe.wait_ge(tok_out, toks.next())
                    return tok[:, n % 2]

                def evicted(name, count):
                    pe.wait_ge(lin_out, i * LIN + (2 + J[name] + count))

                def normalised_to_features(stage):
                    for c in range(C):
                        ps = free_lin()
                        for b in range(PAIR):
                            if c == 0:
                                pe.wait_ge(xn_ready, i * 6 + (PAIR * stage + b + 1))
                            mm = nc.tensor.transpose(ps[:, b * N:(b + 1) * N], xn[:, b, c * P:(c + 1) * P], ident[0:N, 0:N])
                        mm.then_inc(lin_ready, 1)

                def project(wt, m, src, n, chunks):
                    ps = free_lin()
                    for c in range(chunks):
                        mm = nc.tensor.matmul(ps[:, 0:n], wt[:, c, m * P:(m + 1) * P], src[:, c, :],
                                              start=(c == 0), stop=(c == chunks - 1))
                    mm.then_inc(lin_ready, 1)

                def context_keys():
                    for b in range(PAIR):
                        if L == 1:
                            evicted("ctx_t", (b + 1) * CC)
                        for m in range(cw):
                            project(w["ck"], m, ctxT[:, b], M, CC)

                def context_values(b):
                    for m0, mn in MCH:
                        for h in range(parts):
                            ps = free_lin()
                            for c in range(CC):
                                mm = nc.tensor.matmul(ps[0:mn, 0:part_cols], ctxT[:, b, c, m0:m0 + mn],
                                                      w["cv"][:, c, h * part_cols:(h + 1) * part_cols],
                                                      start=(c == 0), stop=(c == CC - 1))
                            mm.then_inc(lin_ready, 1)

                def head_scores(kind, out_ps, b, h):
                    tokens = slice(b * N, (b + 1) * N)
                    if L == 0:
                        c, j = divmod(h, P // hd)
                        q, r = qmask[:, c, j, tokens], slice(0, P)
                    else:
                        c, r = h * hd // P, slice(h * hd % P, h * hd % P + hd)
                        q = qT[r, c, tokens]
                    k = kT[r, c, tokens] if kind == "self" else kc[r, b, c, :]
                    return nc.tensor.matmul(out_ps, q, k, start=True, stop=True)

                def attend(kind):
                    heads, keys, total = HEADS_OF[kind], KEYS_OF[kind], GROUPS_OF[kind]
                    g0 = groups.n
                    part_groups = part_heads // heads
                    for s in range(total + 2):
                        if s < total:
                            n = g0 + s
                            b, hs = group_heads(kind, s)
                            for k, h in enumerate(hs):
                                mm = head_scores(kind, sc[0:N, n % 2, k * keys:(k + 1) * keys], b, h)
                            mm.then_inc(sc_ready, 1)
                            groups.next()
                        if 1 <= s <= total:
                            n = g0 + s - 1
                            pe.wait_ge(prob_ready, groups.at(n + 1))
                            if kind == "self":
                                tiles = [(k * N, N) for k in range(heads)]
                            else:
                                tiles = MCH
                            for t, (m0, mn) in enumerate(tiles):
                                mm = nc.tensor.transpose(tr[0:mn, n % 2, t * N:(t + 1) * N], prob[:, n % 2, m0:m0 + mn],
                                                         ident[0:N, 0:N])
                            mm.then_inc(tr_ready, 1)
                        if s >= 2:
                            g = s - 2
                            n = g0 + g
                            b, hs = group_heads(kind, g)
                            if g % part_groups == 0:
                                ps = free_tok()
                            pe.wait_ge(probT_ready, groups.at(n + 1))
                            for k, h in enumerate(hs):
                                o = h % part_heads * hd
                                f = slice(h * hd, (h + 1) * hd)
                                if kind == "self":
                                    mm = nc.tensor.matmul(ps[0:N, o:o + hd], probT[0:N, n % 2, k * N:(k + 1) * N],
                                                          v_self[:, b, f], start=True, stop=True)
                                else:
                                    for t, (_, mn) in enumerate(MCH):
                                        mm = nc.tensor.matmul(ps[0:N, o:o + hd], probT[0:mn, n % 2, t * N:(t + 1) * N],
                                                              vc[0:mn, b, t, f], start=(t == 0), stop=(t == NM - 1))
                            if (g + 1) % part_groups == 0:
                                mm.then_inc(tok_ready, 1)

                def attention_to_features():
                    before = toks.n - PAIR * parts
                    for b in range(PAIR):
                        for h in range(parts):
                            ps = free_lin()
                            pe.wait_ge(tok_out, toks.at(2 + before + b * parts + h + 1))
                            for c in range(part_chunks):
                                f = (h * part_chunks + c) * P
                                mm = nc.tensor.transpose(ps[:, c * N:(c + 1) * N], o_tok[:, b, f:f + P], ident[0:N, 0:N])
                            mm.then_inc(lin_ready, 1)

                def to_rows(name, per_seq, src, wt, chunks):
                    for b in range(PAIR):
                        ps = free_tok()
                        evicted(name, (b + 1) * per_seq if per_seq else CF)
                        for c in range(chunks):
                            mm = nc.tensor.matmul(ps[0:N, 0:D], src[:, c, b * N:(b + 1) * N], wt[:, c, :],
                                                  start=(c == 0), stop=(c == chunks - 1))
                        mm.then_inc(tok_ready, 1)

                if L == 0:
                    pe.wait_ge(ctx_loaded, i * (16 * ctx_dmas) + 16 * ctx_dmas)
                    context_keys()
                normalised_to_features(0)
                evicted("t0", C)
                for wt in (w_q, w_k):
                    for m in range(cw):
                        project(wt, m, hT, T, C)
                for b in range(PAIR):
                    for h in range(parts):
                        ps = free_lin()
                        for c in range(C):
                            mm = nc.tensor.matmul(ps[0:N, 0:part_cols], hT[:, c, b * N:(b + 1) * N],
                                                  w_v[:, c, h * part_cols:(h + 1) * part_cols],
                                                  start=(c == 0), stop=(c == C - 1))
                        mm.then_inc(lin_ready, 1)
                if L == 1:
                    pe.wait_ge(step, i * VECTOR_MARKS[1] + CTX_MARKS)
                    for b in range(PAIR):
                        for c in range(CC):
                            ps = free_lin()
                            for t, (m0, mn) in enumerate(MCH):
                                mm = nc.tensor.transpose(ps[0:KC, m0:m0 + mn], ctx_in[0:mn, b * NM + t, c * KC:(c + 1) * KC],
                                                         ident[0:mn, 0:mn])
                            mm.then_inc(lin_ready, 1)
                    context_keys()
                    pe.sem_inc(ctx_free, 1)
                context_values(0)
                context_values(1)
                if L == 0:
                    evicted("ctx_v1", NM * parts)
                    pe.sem_inc(ctx_free, 1)
                evicted("v", PAIR * parts)
                pe.wait_ge(q_ready, i * QREADY + (QS if L == 0 else QREADY - QS))
                attend("self")
                attention_to_features()
                to_rows("o1", parts, oT, w["o"], cw)
                normalised_to_features(1)
                evicted("t1", C)
                for m in range(cw):
                    project(w["cq"], m, hT, T, C)
                pe.wait_ge(q_ready, i * QREADY + QREADY)
                evicted("ctx_v1", NM * parts)
                attend("cross")
                attention_to_features()
                to_rows("o2", parts, oT, w["co"], cw)
                normalised_to_features(2)
                evicted("t2", C)
                for m in range(CF):
                    project(w["f1"], m, hT, T, C)
                to_rows("f1", 0, gT, w["f2"], CF)
                for count in (jobs, toks, groups):
                    count.end()


CTX_MARKS = 4 + 2 * PAIR * NM + PAIR * NM


def chunked(w, p=P):
    return np.ascontiguousarray(w.reshape(-1, p, w.shape[1]).transpose(1, 0, 2))


def rotary_columns(w):
    return w.reshape(w.shape[0], H, 2, 16, 2).transpose(0, 1, 2, 4, 3).reshape(w.shape)


def feature_columns(v, p=P):
    v = v.reshape(-1, p).T
    return np.concatenate([v, np.zeros((P - p, v.shape[1]), v.dtype)]) if p < P else v


def rotary_tables():
    freq = (np.float32(1.0) / np.float32(10000.0) ** (np.arange(0, 64, 2, dtype=np.float32) / np.float32(64))).astype(np.float32)
    angle = np.arange(M, dtype=np.float32)[:, None] * freq[None, :]
    row = np.arange(P)
    f = 16 * (row % 64 // 32) + row % 16
    sign = np.where(row % 32 < 16, 1.0, -1.0).astype(np.float32)[:, None]
    return np.cos(angle)[:, f].T.astype(np.float32), (np.sin(angle)[:, f].T * sign).astype(np.float32)


def kernel(**inputs):
    import concourse.bacc as bacc
    from concourse.bass_utils import run_bass_kernel_spmd

    v = {k: np.asarray(x) for k, x in inputs.items()}
    l0 = {k[9:]: x for k, x in v.items() if k.startswith("L0_xcond_")}
    l1 = {k[9:]: x for k, x in v.items() if k.startswith("L1_xcond_")}
    cos, sin = rotary_tables()
    mask = np.kron(np.eye(P // HD[0], dtype=np.float32), np.ones((HD[0], 1), np.float32))
    vectors = {
        "b_ada": [l0["b_ada"]], "b_qkv": [l0["b_qkv"]], "b_ctx": [l0["b_ctx"]], "b_fc1_0": [l0["b_fc1"]],
        "b_fc1_1": [l1["ff_b1"]], "ln_w": [l1["ln1_w"], l1["ln2_w"]], "ln_b": [l1["ln1_b"], l1["ln2_b"]],
        "g_b": [l1["g1_b"], l1["g2_b"]], "beta_b": [l1["b1_b"], l1["b2_b"]],
    }
    cols = [feature_columns(x) for name, _ in COLS[:9] for x in vectors[name]]
    cols += [feature_columns(l1["ca_lnc_w"], KC), feature_columns(l1["ca_lnc_b"], KC), mask]
    arrays = {
        "x": v["x"], "ctx": v["ctx_768"],
        "ctxT": v["ctx_768"].reshape(B, M, CC, KC).transpose(0, 3, 2, 1),
        "condT": chunked(v["cond_1024"].T), "cols": np.concatenate(cols, axis=1),
        "rows": np.stack([l0["b_proj"], l0["b_out"], l0["b_fc2"], l1["sa_bo"], l1["ca_bo"], l1["ff_b2"]]),
        "ident": np.eye(P, dtype=np.float32), "cos": cos, "sin": sin,
        "wada": chunked(l0["W_ada"]),
        "wmod": np.stack([chunked(l1[n]) for n in ("g1_w", "b1_w", "g2_w", "b2_w")], axis=1),
        "wctxT": chunked(l0["W_ctx"].T), "w0_k": chunked(l0["W_k"]), "w0_v": chunked(l0["W_v"]),
        "w0_qkv": chunked(l0["W_qkv"]), "w0_o": chunked(l0["W_proj"]), "w0_cq": chunked(l0["W_q"]),
        "w0_co": chunked(l0["W_out"]), "w0_f1": chunked(l0["W_fc1"]), "w0_f2": chunked(l0["W_fc2"]),
        "w1_q": chunked(rotary_columns(l1["sa_wq"])), "w1_k": chunked(rotary_columns(l1["sa_wkv"][:, :WIDTH[1]])),
        "w1_v": chunked(l1["sa_wkv"][:, WIDTH[1]:]), "w1_o": chunked(l1["sa_wo"]),
        "w1_cq": chunked(rotary_columns(l1["ca_wq"])), "w1_ck": chunked(rotary_columns(l1["ca_wkv"][:, :WIDTH[1]]), KC),
        "w1_cv": chunked(l1["ca_wkv"][:, WIDTH[1]:], KC), "w1_co": chunked(l1["ca_wo"]),
        "w1_f1": chunked(l1["ff_w1"]), "w1_f2": chunked(l1["ff_w2"]),
    }
    nc = bacc.Bacc("TRN2", target_bir_lowering=False, num_devices=1)
    args = {}
    for name in arrays:
        arrays[name] = np.ascontiguousarray(arrays[name])
        args[name] = nc.dram_tensor("in_" + name, arrays[name].shape, F32, kind="ExternalInput").ap()
    out = nc.dram_tensor("out", [B, N, D], F32, kind="ExternalOutput").ap()
    two_blocks(nc, args, out)
    return run_bass_kernel_spmd(nc, [{"in_" + n: x for n, x in arrays.items()}], core_ids=[0]).results[0]["out"]
```

```python
from contextlib import ExitStack

import numpy as np

import concourse.bass as bass
from concourse import mybir

F32 = mybir.dt.float32
ALU = mybir.AluOpType
ACT = mybir.ActivationFunctionType
AX_X = mybir.AxisListType.X

P = 128
B, N, D = 32, 100, 256
M, DC = 361, 192
H = 16
FF = 4 * D
PAIR = 2
ROUNDS = B // PAIR
T = PAIR * N
C = D // P
CF = FF // P
KC = 96
CC = DC // KC
MP = 121
MCH = [(m, min(MP, M - m)) for m in range(0, M, MP)]
NM = len(MCH)
HD = [D // H, 64]
WIDTH = [H * d for d in HD]
CW = [w // P for w in WIDTH]
EPS = [1e-6, 1e-5]
SCALE = [d ** -0.5 for d in HD]
SC_BANKS = 3
LAG = 3
SELF_HEADS = 4
BANK = 512
HEADS_OF = {"self": SELF_HEADS, "cross": 1}
KEYS_OF = {"self": N, "cross": M}
GROUPS_OF = {k: PAIR * H // n for k, n in HEADS_OF.items()}
GROUPS = sum(GROUPS_OF.values())
TOK_PARTS = [1, 2]
TOK_JOBS = [PAIR * (2 * parts + 3) for parts in TOK_PARTS]
NORMS = [3, 4]
ROT = 2
ROTATIONS = (3 + PAIR) * CW[1] // ROT
SWAP = [(p + 16) % 32 for p in range(32)]
KEY_ROTATIONS = PAIR * CW[1] // ROT
CTX_MARKS = 2 * PAIR * NM
MARKS_AHEAD = [2 * PAIR, 2 * PAIR + CTX_MARKS + 3 * KEY_ROTATIONS]
VECTOR_MARKS = [3 * 2 * PAIR + PAIR * 2 * TOK_PARTS[0],
                CTX_MARKS + 3 * 2 * PAIR + PAIR * 2 * TOK_PARTS[1] + 3 * ROTATIONS]

FILLS = [
    {"first": 0, "self": {8: 1, 9: 1}, "b2_t": 2, "b2_q": 1, "b2_s": 3, "cross": {}, "b3_t": 3, "b3_f1": 1, "b3_f2": 0},
    {"first": 8, "self": {8: 1}, "b2_t": 2, "b2_q": 1, "b2_s": 4, "cross": {32: 1, 33: 1}, "b3_t": 3, "b3_f1": 11, "b3_f2": 0},
]
NEXT_ROWS = [(1, 3, 5), (1, 3, 5)]
NEXT_CONTEXT = {"stats": 3, "variance": 3 + PAIR * NM, "norm": 13, "features": 15 + PAIR * NM}

COLS = [("b_ada", 12), ("b_qkv", 6), ("b_ctx", 2), ("b_fc1_0", 8), ("b_fc1_1", 8), ("ln_w", 4), ("ln_b", 4),
        ("g_b", 4), ("beta_b", 4), ("lnc_w", 2), ("lnc_b", 2), ("mask", 8)]
ROWS = 3


def lin_order(L):
    cw, banks = CW[L], TOK_PARTS[L]
    rows = [("next_t", C)] + ([("ctx_t", PAIR * CC)] if L == 1 else [])
    kinds = [("cv", PAIR * NM * banks), ("nv", PAIR * banks), ("nk", PAIR * cw)]
    queue = [(kind, k) for kind, n in kinds for k in range(n)]
    order, places = [], {}

    def fill(place, n):
        places[place] = [queue.pop(0) for _ in range(n)]
        order.extend(places[place])

    def some(name, n):
        order.extend((name, k) for k in range(n))

    f = FILLS[L]
    some("q", cw), some("k", cw), fill("first", f["first"])
    for s in range(GROUPS_OF["self"] + LAG):
        fill(("self", s), f["self"].get(s, 0))
        if s == NEXT_ROWS[L][2]:
            some(*rows[0])
    some("o1", PAIR * banks), fill("b2_t", f["b2_t"]), some("t1", C), fill("b2_q", f["b2_q"]), some("q2", cw)
    fill("b2_s", f["b2_s"])
    assert not [k for k in queue if k[0] == "cv"]
    for s in range(GROUPS_OF["cross"] + LAG):
        fill(("cross", s), f["cross"].get(s, 0))
        if L == 1 and 0 <= s - NEXT_CONTEXT["features"] < PAIR * CC:
            order.append(("ctx_t", s - NEXT_CONTEXT["features"]))
    some("o2", PAIR * banks), fill("b3_t", f["b3_t"]), some("t2", C), fill("b3_f1", f["b3_f1"]), some("f1", CF)
    fill("b3_f2", f["b3_f2"])
    assert not queue
    before = [(name, k) for name, n in rows[0:1] + kinds[1:2] + rows[1:2] + kinds[2:3] for k in range(n)]
    assert len(order) % 2 == 0 and len(before) % 2 == 0
    return {job: n for n, job in enumerate(order)}, len(order), places, {job: n for n, job in enumerate(before)}


class Count:

    def __init__(self, i, per, start=0):
        self.i, self.per, self.start, self.n = i, per, start, 0

    def at(self, n):
        return self.i * self.per + (self.start + n)

    def next(self):
        self.n += 1
        return self.at(self.n)

    def end(self):
        assert self.n == self.per, (self.n, self.per)


def group_heads(kind, g):
    b, h = divmod(g * HEADS_OF[kind], H)
    return b, list(range(h, h + HEADS_OF[kind]))


def spread(ap, shape):
    return ap.rearrange("p (m o) -> p m o", o=1).broadcast_to(shape)


def two_blocks(nc, a, out):
    with ExitStack() as ctx:
        def sb(name, shape):
            return ctx.enter_context(nc.sbuf_tensor(name, list(shape), F32))

        def sem(name):
            return ctx.enter_context(nc.semaphore(name))

        lin, sc, tr, tok = (ctx.enter_context(nc.psum_tensor(n, [P, banks, BANK], F32))
                            for n, banks in (("lin", 2), ("sc", SC_BANKS), ("tr", 1), ("tok", 2)))

        w1 = {n: sb("w1_" + n, a["w1_" + n].shape) for n in ("q", "k", "v", "o", "cq", "ck", "cv", "co", "f1", "f2")}
        cols = sb("cols_sb", [P, sum(n for _, n in COLS)])
        ident, rows = sb("ident_sb", [P, P]), sb("rows_sb", [N, ROWS, D])
        cos, sin = sb("cos_sb", [P, M]), sb("sin_sb", [P, M])
        mod1 = sb("mod1", [P, 8, B + PAIR])
        modcur, modnext = sb("modcur", [P, 12, PAIR]), sb("modnext", [P, 2 * C, PAIR])
        derived = sb("derived", [P, 3, C])
        half = sb("half", [P, 2 * NM])
        norm = {n: sb(n, s) for n, s in (("stats", [P, 6, 6]), ("mv", [P, 6, 2]), ("veps", [P, 6]), ("rstd", [P, 6]))}
        soft = {n: sb(n, [N, PAIR, H]) for n in ("negmax", "sums", "rinv")}
        arena = sb("arena", [P, ARENA])
        used = [0]

        def carve(p, *shape):
            n = int(np.prod(shape))
            ap = arena[0:p, used[0]:used[0] + n]
            used[0] += n
            assert used[0] <= ARENA, used[0]
            dims = "abcd"[:len(shape)]
            if len(shape) > 1:
                ap = ap.rearrange(f"p ({' '.join(dims)}) -> p {' '.join(dims)}", **dict(zip(dims, shape)))
            return ap

        at, pos = {}, 0
        for name, n in COLS:
            at[name] = cols[:, pos:pos + n]
            pos += n
        at["bq"], at["b_ck"], at["b_cv"] = derived[:, 0], derived[:, 1], derived[:, 2]

        x_mid = nc.dram_tensor("x_mid", [B, N, D], F32, kind="Internal").ap()
        w1_loaded = sem("w1_loaded")

        w0 = {n: carve(P, *a["w0_" + n].shape[1:]) for n in ("qkv", "o", "cq", "co", "f1", "f2")}
        w0["ck"], w0["cv"] = carve(KC, CC, D), carve(KC, CC, D)
        mods = [carve(P, 12, B + PAIR), mod1]
        layer0_start = used[0]
        setup(nc, sem, carve, a, at, w0, w1, cols, ident, cos, sin, mods, derived, half, lin, sc, tr, w1_loaded)
        used[0] = layer0_start
        layer(nc, 0, sem, carve, a, at, w0, a["x"], x_mid, ident, rows, mods[0], modcur, modnext, half, norm, soft,
              lin, sc, tr, tok, cos, sin, w1_loaded)
        used[0] = 0
        layer(nc, 1, sem, carve, a, at, w1, x_mid, out, ident, rows, mods[1], modcur, modnext, half, norm, soft,
              lin, sc, tr, tok, cos, sin, w1_loaded)


ARENA = 30540


def setup(nc, sem, carve, a, at, w0, w1, cols, ident, cos, sin, mods, derived, half, lin, sc, tr, w1_loaded):
    wada, wmod = carve(P, C, 12 * P), carve(P, 4, C, D)
    wctxT, wk, wv = carve(P, C, DC), carve(P, C, D), carve(P, C, D)
    condT, silu_c, gain = carve(P, C, B), carve(P, C, B), carve(P, 2, C, B)
    vectors_loaded, factors_loaded, rest_loaded = sem("vectors_loaded"), sem("factors_loaded"), sem("rest_loaded")
    silu_done, folded_out = sem("silu_done"), sem("folded_out")
    mod0_ready, mod1_ready, fold_ready, bias_ready = (sem(n) for n in ("mod0_ready", "mod1_ready", "fold_ready", "bias_ready"))
    step = sem("setup_step")

    with nc.Block() as block:
        @block.sync
        def _(sp):
            sp.dma_start(condT, a["condT"]).then_inc(vectors_loaded, 16)
            sp.dma_start(cols[:], a["cols"]).then_inc(vectors_loaded, 16)
            for dst, name in ((wada, "wada"), (wmod, "wmod"), (wctxT, "wctxT"), (wk, "w0_k"), (wv, "w0_v")):
                sp.dma_start(dst, a[name]).then_inc(factors_loaded, 16)
            loads = [(w0[n], a["w0_" + n]) for n in ("qkv", "o", "cq", "co", "f1", "f2")]
            loads += [(ident[:], a["ident"]), (cos[:], a["cos"]), (sin[:], a["sin"])]
            for dst, src in loads:
                sp.dma_start(dst, src).then_inc(rest_loaded, 16)
            for name, dst in w1.items():
                sp.dma_start(dst[:], a["w1_" + name]).then_inc(w1_loaded, 16)
            sp.wait_ge(rest_loaded, 16 * len(loads))

        @block.scalar
        def _(act):
            act.wait_ge(vectors_loaded, 32)
            nc.scalar.activation(silu_c, condT, ACT.Silu).then_inc(silu_done, 1)
            act.wait_ge(fold_ready, 1)
            for bank, dst in enumerate((w0["ck"], w0["cv"])):
                nc.scalar.copy(dst, sc[0:KC, bank, 0:CC * D].rearrange("p (c n) -> p c n", c=CC)).then_inc(folded_out, 1)
            act.wait_ge(folded_out, 2)

        @block.tensor
        def _(pe):
            pe.wait_ge(silu_done, 1)
            pe.wait_ge(factors_loaded, 80)
            for m in range(12):
                for c in range(C):
                    mm = nc.tensor.matmul(lin[:, 0, m * B:(m + 1) * B], wada[:, c, m * P:(m + 1) * P],
                                          silu_c[:, c, :], start=(c == 0), stop=(c == C - 1))
            mm.then_inc(mod0_ready, 1)
            for k in range(4):
                for m in range(C):
                    o = (k * C + m) * B
                    for c in range(C):
                        mm = nc.tensor.matmul(lin[:, 1, o:o + B], wmod[:, k, c, m * P:(m + 1) * P],
                                              condT[:, c, :], start=(c == 0), stop=(c == C - 1))
            mm.then_inc(mod1_ready, 1)
            for bank, w in enumerate((wk, wv)):
                for r in range(CC):
                    for c in range(C):
                        mm = nc.tensor.matmul(sc[0:KC, bank, r * D:(r + 1) * D], wctxT[:, c, r * KC:(r + 1) * KC],
                                              w[:, c, :], start=(c == 0), stop=(c == C - 1))
            mm.then_inc(fold_ready, 1)
            for j, w in enumerate((wk, wv)):
                for m in range(C):
                    for c in range(C):
                        mm = nc.tensor.matmul(tr[:, 0, C * j + m:C * j + m + 1], w[:, c, m * P:(m + 1) * P],
                                              at["b_ctx"][:, c:c + 1], start=(c == 0), stop=(c == C - 1))
            mm.then_inc(bias_ready, 1)

        @block.vector
        def _(dve):
            done = [0]

            def then_wait(ins):
                done[0] += 1
                ins.then_inc(step, 1)
                dve.wait_ge(step, done[0])

            then_wait(nc.vector.memset(half[:], -0.5))
            for mod in mods:
                then_wait(nc.vector.memset(mod[:, :, B:B + PAIR], 0.0))
            dve.wait_ge(vectors_loaded, 32)
            then_wait(nc.vector.tensor_scalar(derived[:, 0], at["b_qkv"][:, 0:C], SCALE[0], None, ALU.mult))
            dve.wait_ge(mod0_ready, 1)
            then_wait(nc.vector.tensor_tensor(mods[0][:, :, 0:B], lin[:, 0, 0:12 * B].rearrange("p (m b) -> p m b", b=B),
                                              spread(at["b_ada"], [P, 12, B]), ALU.add))
            for s in range(3):
                scale = mods[0][:, 4 * s + C:4 * s + 2 * C, 0:B]
                then_wait(nc.vector.tensor_scalar(scale, scale, 1.0, None, ALU.add))
            dve.wait_ge(mod1_ready, 1)
            for k in range(2):
                g, beta = (lin[:, 1, j * C * B:(j + 1) * C * B].rearrange("p (m b) -> p m b", b=B) for j in (2 * k, 2 * k + 1))
                of = {n: spread(at[n][:, k * C:(k + 1) * C], [P, C, B]) for n in ("g_b", "ln_w", "ln_b", "beta_b")}
                shift, scale = mods[1][:, 4 * k:4 * k + C, 0:B], mods[1][:, 4 * k + C:4 * k + 2 * C, 0:B]
                then_wait(nc.vector.tensor_tensor(gain[:, 0], g, of["g_b"], ALU.add))
                then_wait(nc.vector.tensor_scalar(gain[:, 0], gain[:, 0], 1.0, None, ALU.add))
                then_wait(nc.vector.tensor_tensor(scale, gain[:, 0], of["ln_w"], ALU.mult))
                then_wait(nc.vector.tensor_tensor(gain[:, 1], gain[:, 0], of["ln_b"], ALU.mult))
                then_wait(nc.vector.tensor_tensor(shift, beta, gain[:, 1], ALU.add))
                then_wait(nc.vector.tensor_tensor(shift, shift, of["beta_b"], ALU.add))
            dve.wait_ge(bias_ready, 1)
            then_wait(nc.vector.tensor_copy(derived[:, 1:3], tr[:, 0, 0:2 * C].rearrange("p (j c) -> p j c", c=C)))


def layer(nc, L, sem_of, carve, a, at, w, x_src, x_dst, ident, rows, mod, modcur, modnext, half, norm, soft,
          lin, sc, tr, tok, cos, sin, w1_loaded):
    hd, cw, width, parts = HD[L], CW[L], WIDTH[L], TOK_PARTS[L]
    stats, mv, veps, rstd = (norm[n] for n in ("stats", "mv", "veps", "rstd"))
    negmax, sums, rinv = (soft[n] for n in ("negmax", "sums", "rinv"))
    J, LIN, PLACES, J_AHEAD = lin_order(L)
    AHEAD = len(J_AHEAD)
    TOK, MARKS = TOK_JOBS[L], VECTOR_MARKS[L]
    QREADY = 2 * cw if L == 0 else ROTATIONS
    QAHEAD = 0 if L == 0 else KEY_ROTATIONS
    Q2READY = cw if L == 0 else cw // ROT
    part_heads = H // parts
    part_cols = width // parts
    part_chunks = cw // parts
    w_q = w["qkv"][:, :, 0:D] if L == 0 else w["q"]
    w_k = w["qkv"][:, :, D:2 * D] if L == 0 else w["k"]
    w_v = w["qkv"][:, :, 2 * D:3 * D] if L == 0 else w["v"]
    ctx_values = [(b, t, h) for b in range(PAIR) for t in range(NM) for h in range(parts)]
    own_values = [(b, h) for b in range(PAIR) for h in range(parts)]
    key_chunks = [(b, m) for b in range(PAIR) for m in range(cw)]

    def sem(name):
        return sem_of(f"{name}_{L}")

    x_in = carve(N, PAIR, D)
    x_now = carve(N, PAIR, D)
    x_bias = carve(N, PAIR, D)
    xn = carve(N, PAIR, D)
    hT = carve(P, C, T)
    hT0 = carve(P, C, T)
    qT, kT = carve(P, cw, T), carve(P, cw, T)
    qmask = carve(P, cw, P // hd, T)
    v_self = carve(N, PAIR, width)
    kc = carve(P, PAIR, cw, M)
    vc = carve(MP, PAIR, NM, width)
    ctxT = carve(KC, PAIR, CC, M)
    prob = carve(N, SC_BANKS, 400)
    shared = carve(P, 2 * 400)
    probT = shared[0:MP].rearrange("p (two n) -> p two n", two=2)
    o_tok = carve(N, PAIR, width)
    oT = kT
    if L == 0:
        gT = carve(P, CF, T)
    else:
        gT = qT
        ctx_in = carve(MP, PAIR * NM, DC)
        swapped = shared

    x_loaded, ctx_loaded, x_stored, rows_loaded = (sem(n) for n in ("x_loaded", "ctx_loaded", "x_stored", "rows_loaded"))
    x_in_free, ctx_free = sem("x_in_free"), sem("ctx_free")
    ctx_rows = sem("ctx_rows")
    lin_ready, lin_out = sem("lin_ready"), sem("lin_out")
    tok_ready, tok_out = sem("tok_ready"), sem("tok_out")
    sc_ready, max_ready, prob_ready = sem("sc_ready"), sem("max_ready"), sem("prob_ready")
    tr_ready, probT_ready = sem("tr_ready"), sem("probT_ready")
    var_ready, rstd_ready, xn_ready = sem("var_ready"), sem("rstd_ready"), sem("xn_ready")
    bias_added, mod_ready = sem("bias_added"), sem("mod_ready")
    q_ready = sem("q_ready")
    cleared, step, stats_seen = sem("cleared"), sem("vector_step"), sem("stats_seen")
    ctx_dmas = PAIR if L == 0 else 2 * PAIR

    with nc.Block() as block:
        @block.sync
        def _(sp):
            def load_x(pair):
                sp.dma_start(x_in, x_src[bass.ds(pair * PAIR, PAIR)].rearrange("b n d -> n b d")).then_inc(x_loaded, 16)

            def load_context(pair):
                for b in range(PAIR):
                    if L == 0:
                        sp.dma_start(ctxT[:, b], a["ctxT"][bass.ds(pair * PAIR + b, 1)].rearrange("o p c m -> (o p) c m"))\
                          .then_inc(ctx_loaded, 16)
                    else:
                        src = a["ctx"][bass.ds(pair * PAIR + b, 1)].rearrange("o m d -> (o m) d")
                        whole, rest = MCH[-1]
                        sp.dma_start(ctx_in[:, b * NM:b * NM + NM - 1, :],
                                     src[0:whole].rearrange("(t p) d -> p t d", p=MP)).then_inc(ctx_loaded, 16)
                        sp.dma_start(ctx_in[0:rest, b * NM + NM - 1, :], src[whole:M]).then_inc(ctx_loaded, 16)

            def store(pair):
                sp.wait_ge(tok_out, pair * TOK + (2 + TOK))
                sp.dma_start(x_dst[bass.ds(pair * PAIR, PAIR)].rearrange("b n d -> n b d"), x_now).then_inc(x_stored, 16)

            sp.sem_inc(x_stored, 16)
            load_x(0)
            sp.dma_start(rows[:], a["rows"][L].partition_broadcast(N)).then_inc(rows_loaded, 16)
            if L == 1:
                sp.wait_ge(cleared, 1)
            load_context(0)
            with nc.Fori(0, ROUNDS - 1, engines=[sp.engine]) as i:
                sp.wait_ge(x_in_free, i + 1)
                load_x(i + 1)
                sp.wait_ge(ctx_free, i + 1)
                load_context(i + 1)
                store(i)
            sp.wait_ge(x_in_free, ROUNDS)
            load_x(0)
            sp.wait_ge(ctx_free, ROUNDS)
            load_context(0)
            store(ROUNDS - 1)
            sp.wait_ge(x_stored, 16 * (ROUNDS + 1))

        @block.gpsimd
        def _(pool):
            def inverse_root(value, p, n):
                pool.wait_ge(var_ready, value)
                nc.gpsimd.tensor_tensor(rstd[0:p, 0:n], veps[0:p, 0:n], half[0:p, 0:n], ALU.pow).then_inc(rstd_ready, 1)

            nc.gpsimd.tensor_copy(modnext[:], mod[:, 0:2 * C, 0:PAIR]).then_inc(mod_ready, 1)
            inverse_root(1, N, PAIR)
            if L == 1:
                inverse_root(2, MP, PAIR * NM)
            pool.wait_ge(rows_loaded, 16)
            with nc.Fori(0, ROUNDS, engines=[pool.engine]) as i:
                roots = Count(i, NORMS[L], 1 + L)
                pool.wait_ge(lin_out, i * LIN + (2 + AHEAD))
                n_mod = mod.shape[1]
                nc.gpsimd.tensor_copy(modcur[:, 0:n_mod, :], mod[:, :, bass.ds(i * PAIR, PAIR)])
                nc.gpsimd.tensor_copy(modnext[:], mod[:, 0:2 * C, bass.ds(i * PAIR + PAIR, PAIR)]).then_inc(mod_ready, 1)

                def add_bias(src, r):
                    nc.gpsimd.tensor_tensor(x_bias, src, rows[:, r:r + 1, :].broadcast_to([N, PAIR, D]), ALU.add)\
                      .then_inc(bias_added, 1)

                pool.wait_ge(x_loaded, i * 16 + 16)
                add_bias(x_in, 0)
                pool.wait_ge(xn_ready, i * 6 + 2)
                pool.wait_ge(bias_added, i * 3 + 1)
                pool.sem_inc(x_in_free, 1)
                inverse_root(roots.next(), N, PAIR)
                inverse_root(roots.next(), N, PAIR)
                add_bias(x_now, 1)
                if L == 1:
                    inverse_root(roots.next(), MP, PAIR * NM)
                inverse_root(roots.next(), N, PAIR)
                add_bias(x_now, 2)
                roots.end()
                pool.wait_ge(tok_out, i * TOK + (2 + TOK))

        @block.scalar
        def _(act):
            act.sem_inc(lin_out, 2)

            def bank_of(n, value):
                act.wait_ge(lin_ready, value)
                return lin[:, n % 2]

            def evict_modulated(take, dst, mods, s):
                for c in range(C):
                    ps = take()
                    for b in range(PAIR):
                        ins = nc.scalar.activation(dst[:, c, b * N:(b + 1) * N], ps[:, b * N:(b + 1) * N], ACT.Identity,
                                                   bias=mods[:, s + c, b:b + 1], scale=mods[:, s + C + c, b:b + 1])
                    ins.then_inc(lin_out, 1)

            def evict_context(take, k):
                b, c = divmod(k, CC)
                ps = take()
                nc.scalar.activation(ctxT[:, b, c, :], ps[0:KC, 0:M], ACT.Identity, bias=at["lnc_b"][0:KC, c:c + 1],
                                     scale=at["lnc_w"][0:KC, c:c + 1]).then_inc(lin_out, 1)

            def evict_fills(take, jobs):
                for kind, k in jobs:
                    ps = take()
                    if kind == "cv":
                        b, t, h = ctx_values[k]
                        mn = MCH[t][1]
                        ins = nc.scalar.copy(vc[0:mn, b, t, h * part_cols:(h + 1) * part_cols], ps[0:mn, 0:part_cols])
                    elif kind == "nv":
                        b, h = own_values[k]
                        ins = nc.scalar.copy(v_self[:, b, h * part_cols:(h + 1) * part_cols], ps[0:N, 0:part_cols])
                    else:
                        b, m = key_chunks[k]
                        if L == 0:
                            ins = nc.scalar.activation(kc[:, b, m, :], ps[:, 0:M], ACT.Identity, bias=at["b_ck"][:, m:m + 1])
                        else:
                            ins = nc.scalar.copy(kc[:, b, m, :], ps[:, 0:M])
                    ins.then_inc(lin_out, 1)

            ahead = [0]

            def take_ahead():
                ahead[0] += 1
                return bank_of(ahead[0] - 1, ahead[0])

            act.wait_ge(mod_ready, 1)
            evict_modulated(take_ahead, hT0, modnext, 0)
            evict_fills(take_ahead, [job for job in J_AHEAD if job[0] == "nv"])
            if L == 1:
                for k in range(PAIR * CC):
                    evict_context(take_ahead, k)
            evict_fills(take_ahead, [job for job in J_AHEAD if job[0] == "nk"])
            assert ahead[0] == AHEAD

            with nc.Fori(0, ROUNDS, engines=[act.engine]) as i:
                filled = Count(i, LIN, AHEAD)
                maxima = Count(i, GROUPS)

                def take():
                    n = filled.n
                    return bank_of(n, filled.next())

                def evict_chunks(dst, n, scale, bias=None):
                    for c in range(cw):
                        ps = take()
                        if bias is None:
                            nc.scalar.activation(dst[:, c, :], ps[:, 0:n], ACT.Copy, scale=scale).then_inc(lin_out, 1)
                        else:
                            nc.scalar.activation(dst[:, c, :], ps[:, 0:n], ACT.Identity, scale=scale,
                                                 bias=bias[:, c:c + 1]).then_inc(lin_out, 1)

                def probabilities(kind, beside={}):
                    keys = KEYS_OF[kind]
                    for g in range(GROUPS_OF[kind] + LAG):
                        if g < GROUPS_OF[kind]:
                            n = maxima.n
                            b, hs = group_heads(kind, g)
                            act.wait_ge(max_ready, maxima.next())
                            for k, h in enumerate(hs):
                                ins = nc.scalar.activation(prob[:, n % SC_BANKS, k * keys:(k + 1) * keys],
                                                           sc[0:N, n % SC_BANKS, k * keys:(k + 1) * keys], ACT.Exp,
                                                           bias=negmax[:, b, h:h + 1], accum_out=sums[:, b, h:h + 1])
                            ins.then_inc(prob_ready, 1)
                        evict_fills(take, PLACES[kind, g])
                        if g in beside:
                            beside[g]()

                def evict_attention(bias):
                    for b in range(PAIR):
                        for h in range(parts):
                            ps = take()[:, 0:part_chunks * N].rearrange("p (c n) -> p c n", n=N)
                            dst = oT[:, h * part_chunks:(h + 1) * part_chunks, b * N:(b + 1) * N]
                            if bias is None:
                                ins = nc.scalar.copy(dst, ps)
                            else:
                                for c in range(part_chunks):
                                    ins = nc.scalar.activation(dst[:, c], ps[:, c], ACT.Identity, bias=bias[:, c:c + 1])
                            ins.then_inc(lin_out, 1)

                evict_chunks(qT, T, SCALE[L], at["bq"] if L == 0 else None)
                evict_chunks(kT, T, 1.0, at["b_qkv"][:, C:2 * C] if L == 0 else None)
                evict_fills(take, PLACES["first"])
                act.wait_ge(mod_ready, i + 2)
                probabilities("self", {NEXT_ROWS[L][2]: lambda: evict_modulated(take, hT0, modnext, 0)})
                evict_attention(at["b_qkv"][:, 2 * C:3 * C] if L == 0 else None)
                evict_fills(take, PLACES["b2_t"])
                evict_modulated(take, hT, modcur, 2 * C if L == 0 else 0)
                evict_fills(take, PLACES["b2_q"])
                evict_chunks(qT, T, SCALE[L])
                evict_fills(take, PLACES["b2_s"])
                probabilities("cross", {NEXT_CONTEXT["features"] + k: lambda k=k: evict_context(take, k)
                                        for k in range(PAIR * CC)} if L == 1 else {})
                evict_attention(at["b_cv"] if L == 0 else None)
                evict_fills(take, PLACES["b3_t"])
                evict_modulated(take, hT, modcur, 4 * C if L == 0 else 2 * C)
                evict_fills(take, PLACES["b3_f1"])
                for m in range(CF):
                    ps = take()
                    nc.scalar.activation(gT[:, m, :], ps[:, 0:T], ACT.Gelu_apprx_tanh if L == 0 else ACT.Gelu,
                                         bias=at[f"b_fc1_{L}"][:, m:m + 1]).then_inc(lin_out, 1)
                evict_fills(take, PLACES["b3_f2"])
                filled.end()
                maxima.end()

        @block.vector
        def _(dve):
            if L == 1:
                nc.vector.memset(ctx_in, 0.0)
                nc.vector.memset(qmask, 0.0)
            nc.vector.memset(tr[:], 0.0).then_inc(cleared, 1)
            dve.sem_inc(tok_out, 2)

            def variance(mark, src, p, n):
                first = [mark(nc.vector.bn_stats(stats[0:p, s, :], src[:, s])) for s in range(n)]
                aggregated(mark, first[-1], p, n)

            def aggregated(mark, stats_there, p, n):
                dve.wait_ge(step, stats_there)
                dve.sem_inc(stats_seen, 1)
                for s in range(n):
                    last = mark(nc.vector.bn_aggr(mv[0:p, s, :], stats[0:p, s, :]))
                dve.wait_ge(step, last)
                nc.vector.tensor_scalar(veps[0:p, 0:n], mv[0:p, 0:n, 1], EPS[L], None, ALU.add).then_inc(var_ready, 1)

            def normalise_tile(s, src, dst, p):
                return nc.vector.tensor_scalar(dst[:, s], src[:, s], mv[0:p, s, 0:1], rstd[0:p, s:s + 1],
                                               ALU.subtract, ALU.mult)

            def normalised(value, src, dst, p, n, done):
                dve.wait_ge(rstd_ready, value)
                for s in range(n):
                    done(normalise_tile(s, src, dst, p))

            marked = [0]

            def mark_ahead(ins):
                marked[0] += 1
                ins.then_inc(step, 1)
                return marked[0]

            def rotate(marked_by, value, after, chunk0, n, reps, into=None):
                def runs(ap):
                    return ap.rearrange("p (r n) -> p r n", n=n)

                def table(t):
                    return t[:, 0:n].unsqueeze(1).broadcast_to([P, reps, n])

                buf = chunk0.rearrange("p c t -> p (c t)")
                sw = swapped[:, 0:reps * n]
                dve.wait_ge(lin_out, after)
                by_sin = marked_by(nc.vector.tensor_tensor(runs(sw), runs(buf), table(sin), ALU.mult))
                dve.wait_ge(step, by_sin)
                marked_by(nc.vector.tensor_tensor(runs(buf), runs(buf), table(cos), ALU.mult))
                shuffled = marked_by(nc.vector.stream_shuffle(sw, sw, SWAP))
                dve.wait_ge(step, shuffled)
                if into is None:
                    nc.vector.tensor_tensor(buf, buf, sw, ALU.add).then_inc(q_ready, 1)
                else:
                    for j in range(P // hd):
                        r = slice(j * hd, (j + 1) * hd)
                        ins = nc.vector.tensor_tensor(into[r, :, j, :], chunk0[r],
                                                      sw[r].rearrange("p (c t) -> p c t", c=ROT), ALU.add)
                    ins.then_inc(q_ready, 1)
                dve.wait_ge(q_ready, value)

            def rotate_context_keys(marked_by, value_of, after_of):
                for k in range(0, PAIR * cw, ROT):
                    b, m = key_chunks[k]
                    rotate(marked_by, value_of(), after_of(k + ROT - 1), kc[:, b, m:m + ROT, :], M, ROT)

            dve.wait_ge(x_loaded, 16)
            variance(mark_ahead, x_in, N, PAIR)
            normalised(1, x_in, xn, N, PAIR, lambda ins: ins.then_inc(xn_ready, 1))
            if L == 1:
                rotated = [0]

                def rotated_next():
                    rotated[0] += 1
                    return rotated[0]

                dve.wait_ge(ctx_loaded, 16 * ctx_dmas)
                variance(mark_ahead, ctx_in, MP, PAIR * NM)
                normalised(2, ctx_in, ctx_in, MP, PAIR * NM, lambda ins: ins.then_inc(ctx_rows, 1))
                rotate_context_keys(mark_ahead, rotated_next, lambda k: 2 + J_AHEAD["nk", k] + 1)
            assert marked[0] == MARKS_AHEAD[L]

            with nc.Fori(0, ROUNDS, engines=[dve.engine]) as i:
                marks = Count(i, MARKS, MARKS_AHEAD[L])
                toks = Count(i, TOK)
                groups = Count(i, GROUPS)
                roots = Count(i, NORMS[L], 1 + L)
                chunks = Count(i, QREADY, QAHEAD)

                def mark(ins):
                    ins.then_inc(step, 1)
                    return marks.next()

                def evicted(*job):
                    return i * LIN + (2 + AHEAD + J[job] + 1)

                def rows_normalised(src):
                    normalised(roots.next(), src, xn, N, PAIR, lambda ins: ins.then_inc(xn_ready, 1))

                def mask_queries(name):
                    for c in range(cw):
                        dve.wait_ge(lin_out, evicted(name, c))
                        nc.vector.tensor_tensor(qmask[:, c], qT[:, c:c + 1, :].broadcast_to([P, P // hd, T]),
                                                spread(at["mask"], [P, P // hd, T]), ALU.mult).then_inc(q_ready, 1)
                        chunks.next()

                def rotate_tokens(src, name, masked):
                    for c in range(0, cw, ROT):
                        rotate(mark, chunks.next(), evicted(name, c + ROT - 1), src[:, c:c + ROT, :], N, ROT * PAIR,
                               qmask[:, c:c + ROT] if masked else None)

                def attend(kind, beside={}):
                    heads, keys, total = HEADS_OF[kind], KEYS_OF[kind], GROUPS_OF[kind]
                    g0 = groups.n
                    part_groups = part_heads // heads
                    for s in range(total + LAG + 1):
                        if s < total:
                            n = g0 + s
                            b, hs = group_heads(kind, s)
                            dve.wait_ge(sc_ready, groups.next())
                            nc.vector.tensor_reduce(negmax[:, b, hs[0]:hs[-1] + 1],
                                                    sc[0:N, n % SC_BANKS, 0:heads * keys].rearrange("p (h k) -> p h k", h=heads),
                                                    AX_X, ALU.max, negate=True).then_inc(max_ready, 1)
                        if 2 <= s <= total + 1:
                            n = g0 + s - 2
                            p, used = (N, heads * N) if kind == "self" else (MP, NM * N)
                            dve.wait_ge(tr_ready, groups.at(n + 1))
                            nc.vector.tensor_copy(probT[0:p, n % 2, 0:used], tr[0:p, 0, 0:used]).then_inc(probT_ready, 1)
                        if s > LAG and (s - LAG) % part_groups == 0:
                            b, part = divmod((s - LAG) // part_groups - 1, parts)
                            hs = slice(part * part_heads, (part + 1) * part_heads)
                            bank = toks.n % 2
                            dve.wait_ge(tok_ready, toks.next())
                            inverted = mark(nc.vector.reciprocal(rinv[:, b, hs], sums[:, b, hs]))
                            dve.wait_ge(step, inverted)
                            nc.vector.tensor_tensor(
                                o_tok[:, b, part * part_cols:(part + 1) * part_cols].rearrange("p (h d) -> p h d", d=hd),
                                tok[0:N, bank, 0:part_cols].rearrange("p (h d) -> p h d", d=hd),
                                spread(rinv[:, b, hs], [N, part_heads, hd]), ALU.mult).then_inc(tok_out, 1)
                        if s in beside:
                            beside[s]()

                def add_residual(stage):
                    dve.wait_ge(bias_added, i * 3 + (stage + 1))
                    if stage == 0:
                        dve.wait_ge(x_stored, i * 16 + 16)
                    for b in range(PAIR):
                        bank = toks.n % 2
                        dve.wait_ge(tok_ready, toks.next())
                        nc.vector.tensor_tensor(x_now[:, b], tok[0:N, bank, 0:D], x_bias[:, b], ALU.add).then_inc(tok_out, 1)
                    dve.wait_ge(tok_out, toks.at(toks.n + 2))

                def next_variance():
                    dve.wait_ge(x_loaded, i * 16 + 32)
                    variance(mark, x_in, N, PAIR)

                def next_context():
                    at_slot = {}
                    for t in range(PAIR * NM):
                        def tile_stats(t=t):
                            if t == 0:
                                dve.wait_ge(ctx_loaded, i * (16 * ctx_dmas) + 32 * ctx_dmas)
                            stats_at.append(mark(nc.vector.bn_stats(stats[0:MP, t, :], ctx_in[:, t])))

                        def tile_normalised(t=t):
                            if t == 0:
                                dve.wait_ge(rstd_ready, roots.next())
                            normalise_tile(t, ctx_in, ctx_in, MP).then_inc(ctx_rows, 1)

                        at_slot[NEXT_CONTEXT["stats"] + t] = tile_stats
                        at_slot[NEXT_CONTEXT["norm"] + t] = tile_normalised
                    stats_at = []
                    at_slot[NEXT_CONTEXT["variance"]] = lambda: aggregated(mark, stats_at[-1], MP, PAIR * NM)
                    return at_slot

                if L == 0:
                    mask_queries("q")
                else:
                    rotate_tokens(qT, "q", True)
                    rotate_tokens(kT, "k", False)
                attend("self", {NEXT_ROWS[L][0]: next_variance, NEXT_ROWS[L][1]: lambda: rows_normalised(x_in)})
                add_residual(0)
                variance(mark, x_now, N, PAIR)
                rows_normalised(x_now)
                if L == 0:
                    mask_queries("q2")
                else:
                    rotate_tokens(qT, "q2", True)
                attend("cross", next_context() if L == 1 else {})
                add_residual(1)
                variance(mark, x_now, N, PAIR)
                rows_normalised(x_now)
                if L == 1:
                    rotate_context_keys(mark, chunks.next, lambda k: evicted("nk", k))
                add_residual(2)
                for count in (marks, toks, groups, roots, chunks):
                    count.end()

        @block.tensor
        def _(pe):
            if L == 1:
                pe.wait_ge(w1_loaded, 16 * len(w))
            pe.wait_ge(cleared, 1)

            def bank_of(n, value):
                pe.wait_ge(lin_out, value)
                return lin[:, n % 2]

            def normalised_to_features(take, first):
                for c in range(C):
                    ps = take()
                    for b in range(PAIR):
                        if c == 0:
                            pe.wait_ge(xn_ready, first + b)
                        mm = nc.tensor.transpose(ps[:, b * N:(b + 1) * N], xn[:, b, c * P:(c + 1) * P], ident[0:N, 0:N])
                    mm.then_inc(lin_ready, 1)

            def context_to_features(take, k, value):
                b, c = divmod(k, CC)
                ps = take()
                pe.wait_ge(ctx_rows, value)
                for t, (m0, mn) in enumerate(MCH):
                    mm = nc.tensor.transpose(ps[0:KC, m0:m0 + mn], ctx_in[0:mn, b * NM + t, c * KC:(c + 1) * KC],
                                             ident[0:mn, 0:mn])
                mm.then_inc(lin_ready, 1)

            def fill(take, jobs):
                for kind, k in jobs:
                    ps = take()
                    if kind == "cv":
                        b, t, h = ctx_values[k]
                        m0, mn = MCH[t]
                        for c in range(CC):
                            mm = nc.tensor.matmul(ps[0:mn, 0:part_cols], ctxT[:, b, c, m0:m0 + mn],
                                                  w["cv"][:, c, h * part_cols:(h + 1) * part_cols],
                                                  start=(c == 0), stop=(c == CC - 1))
                    elif kind == "nv":
                        b, h = own_values[k]
                        for c in range(C):
                            mm = nc.tensor.matmul(ps[0:N, 0:part_cols], hT0[:, c, b * N:(b + 1) * N],
                                                  w_v[:, c, h * part_cols:(h + 1) * part_cols],
                                                  start=(c == 0), stop=(c == C - 1))
                    else:
                        b, m = key_chunks[k]
                        for c in range(CC):
                            mm = nc.tensor.matmul(ps[:, 0:M], w["ck"][:, c, m * P:(m + 1) * P], ctxT[:, b, c, :],
                                                  start=(c == 0), stop=(c == CC - 1))
                    mm.then_inc(lin_ready, 1)

            ahead = [0]

            def take_ahead():
                ahead[0] += 1
                return bank_of(ahead[0] - 1, ahead[0])

            normalised_to_features(take_ahead, 1)
            pe.wait_ge(lin_out, 2 + C)
            fill(take_ahead, [job for job in J_AHEAD if job[0] == "nv"])
            if L == 1:
                for k in range(PAIR * CC):
                    context_to_features(take_ahead, k, PAIR * NM)
                pe.wait_ge(lin_out, 2 + J_AHEAD["ctx_t", PAIR * CC - 1] + 1)
                pe.sem_inc(ctx_free, 1)
            else:
                pe.wait_ge(ctx_loaded, 16 * ctx_dmas)
            fill(take_ahead, [job for job in J_AHEAD if job[0] == "nk"])

            with nc.Fori(0, ROUNDS, engines=[pe.engine], hint_back_edge=True) as i:
                jobs = Count(i, LIN, AHEAD)
                toks = Count(i, TOK)
                groups = Count(i, GROUPS)

                def take():
                    n = jobs.n
                    return bank_of(n, jobs.next())

                def free_tok():
                    n = toks.n
                    pe.wait_ge(tok_out, toks.next())
                    return tok[:, n % 2]

                def evicted(*job):
                    pe.wait_ge(lin_out, i * LIN + (2 + AHEAD + J[job] + 1))

                def project(wt, m, src, n, chunks):
                    ps = take()
                    for c in range(chunks):
                        mm = nc.tensor.matmul(ps[:, 0:n], wt[:, c, m * P:(m + 1) * P], src[:, c, :],
                                              start=(c == 0), stop=(c == chunks - 1))
                    mm.then_inc(lin_ready, 1)

                def attend(kind, beside={}):
                    heads, keys, total = HEADS_OF[kind], KEYS_OF[kind], GROUPS_OF[kind]
                    g0 = groups.n
                    part_groups = part_heads // heads
                    for s in range(total + LAG):
                        if s < total:
                            n = g0 + s
                            b, hs = group_heads(kind, s)
                            for k, h in enumerate(hs):
                                c, j = divmod(h, P // hd)
                                tokens = slice(b * N, (b + 1) * N)
                                mm = nc.tensor.matmul(sc[0:N, n % SC_BANKS, k * keys:(k + 1) * keys], qmask[:, c, j, tokens],
                                                      kT[:, c, tokens] if kind == "self" else kc[:, b, c, :],
                                                      start=True, stop=True)
                            mm.then_inc(sc_ready, 1)
                            groups.next()
                        fill(take, PLACES[kind, s])
                        if s in beside:
                            beside[s]()
                        if 2 <= s <= total + 1:
                            n = g0 + s - 2
                            pe.wait_ge(prob_ready, groups.at(n + 1))
                            if s > 2:
                                pe.wait_ge(probT_ready, groups.at(n))
                            tiles = [(k * N, N) for k in range(heads)] if kind == "self" else MCH
                            for t, (m0, mn) in enumerate(tiles):
                                mm = nc.tensor.transpose(tr[0:mn, 0, t * N:(t + 1) * N], prob[:, n % SC_BANKS, m0:m0 + mn],
                                                         ident[0:N, 0:N])
                            mm.then_inc(tr_ready, 1)
                        if s >= LAG:
                            g = s - LAG
                            n = g0 + g
                            b, hs = group_heads(kind, g)
                            if g % part_groups == 0:
                                ps = free_tok()
                            pe.wait_ge(probT_ready, groups.at(n + 1))
                            for k, h in enumerate(hs):
                                o = h % part_heads * hd
                                f = slice(h * hd, (h + 1) * hd)
                                if kind == "self":
                                    mm = nc.tensor.matmul(ps[0:N, o:o + hd], probT[0:N, n % 2, k * N:(k + 1) * N],
                                                          v_self[:, b, f], start=True, stop=True)
                                else:
                                    for t, (_, mn) in enumerate(MCH):
                                        mm = nc.tensor.matmul(ps[0:N, o:o + hd], probT[0:mn, n % 2, t * N:(t + 1) * N],
                                                              vc[0:mn, b, t, f], start=(t == 0), stop=(t == NM - 1))
                            if (g + 1) % part_groups == 0:
                                mm.then_inc(tok_ready, 1)

                def attention_to_features():
                    before = toks.n - PAIR * parts
                    for b in range(PAIR):
                        for h in range(parts):
                            ps = take()
                            pe.wait_ge(tok_out, toks.at(2 + before + b * parts + h + 1))
                            for c in range(part_chunks):
                                f = (h * part_chunks + c) * P
                                mm = nc.tensor.transpose(ps[:, c * N:(c + 1) * N], o_tok[:, b, f:f + P], ident[0:N, 0:N])
                            mm.then_inc(lin_ready, 1)

                def to_rows(name, per_seq, src, wt, chunks):
                    for b in range(PAIR):
                        ps = free_tok()
                        if per_seq:
                            evicted(name, (b + 1) * per_seq - 1)
                        for c in range(chunks):
                            if not per_seq and b == 0:
                                evicted(name, c)
                            mm = nc.tensor.matmul(ps[0:N, 0:D], src[:, c, b * N:(b + 1) * N], wt[:, c, :],
                                                  start=(c == 0), stop=(c == chunks - 1))
                        mm.then_inc(tok_ready, 1)

                for wt in (w_q, w_k):
                    for m in range(cw):
                        project(wt, m, hT0, T, C)
                fill(take, PLACES["first"])
                evicted("k", cw - 1)
                pe.wait_ge(q_ready, i * QREADY + (QAHEAD + (cw if L == 0 else 2 * cw // ROT)))
                attend("self", {NEXT_ROWS[L][2]: lambda: normalised_to_features(take, i * 6 + 3)})
                attention_to_features()
                to_rows("o1", parts, oT, w["o"], cw)
                evicted("next_t", C - 1)
                fill(take, PLACES["b2_t"])
                normalised_to_features(take, i * 6 + 5)
                fill(take, PLACES["b2_q"])
                evicted("t1", C - 1)
                for m in range(cw):
                    project(w["cq"], m, hT, T, C)
                fill(take, PLACES["b2_s"])
                evicted("cv", len(ctx_values) - 1)
                if L == 0:
                    pe.sem_inc(ctx_free, 1)
                pe.wait_ge(q_ready, i * QREADY + (QAHEAD + (cw if L == 0 else 2 * cw // ROT) + Q2READY))
                if L == 1:
                    next_context = {NEXT_CONTEXT["features"] + k:
                                    lambda k=k: context_to_features(take, k, i * (PAIR * NM) + 2 * PAIR * NM)
                                    for k in range(PAIR * CC)}
                else:
                    next_context = {GROUPS_OF["cross"] - 1:
                                    lambda: pe.wait_ge(ctx_loaded, i * (16 * ctx_dmas) + 32 * ctx_dmas)}
                attend("cross", next_context)
                attention_to_features()
                if L == 1:
                    evicted("ctx_t", PAIR * CC - 1)
                    pe.sem_inc(ctx_free, 1)
                to_rows("o2", parts, oT, w["co"], cw)
                fill(take, PLACES["b3_t"])
                normalised_to_features(take, i * 6 + 7)
                fill(take, PLACES["b3_f1"])
                evicted("t2", C - 1)
                for m in range(CF):
                    project(w["f1"], m, hT, T, C)
                fill(take, PLACES["b3_f2"])
                to_rows("f1", 0, gT, w["f2"], CF)
                for count in (jobs, toks, groups):
                    count.end()


def chunked(w, p=P):
    return np.ascontiguousarray(w.reshape(-1, p, w.shape[1]).transpose(1, 0, 2))


def rotary_columns(w):
    return w.reshape(w.shape[0], H, 2, 16, 2).transpose(0, 1, 2, 4, 3).reshape(w.shape)


def feature_columns(v, p=P):
    v = v.reshape(-1, p).T
    return np.concatenate([v, np.zeros((P - p, v.shape[1]), v.dtype)]) if p < P else v


def rotary_tables():
    freq = (np.float32(1.0) / np.float32(10000.0) ** (np.arange(0, 64, 2, dtype=np.float32) / np.float32(64))).astype(np.float32)
    angle = np.arange(M, dtype=np.float32)[:, None] * freq[None, :]
    row = np.arange(P)
    f = 16 * (row % 64 // 32) + row % 16
    sign = np.where(row % 32 < 16, 1.0, -1.0).astype(np.float32)[:, None]
    return np.cos(angle)[:, f].T.astype(np.float32), (np.sin(angle)[:, f].T * sign).astype(np.float32)


def kernel(**inputs):
    import concourse.bacc as bacc
    from concourse.bass_utils import run_bass_kernel_spmd

    v = {k: np.asarray(x) for k, x in inputs.items()}
    l0 = {k[9:]: x for k, x in v.items() if k.startswith("L0_xcond_")}
    l1 = {k[9:]: x for k, x in v.items() if k.startswith("L1_xcond_")}
    cos, sin = rotary_tables()
    mask = np.kron(np.eye(P // HD[0], dtype=np.float32), np.ones((HD[0], 1), np.float32))
    vectors = {
        "b_ada": [l0["b_ada"]], "b_qkv": [l0["b_qkv"]], "b_ctx": [l0["b_ctx"]], "b_fc1_0": [l0["b_fc1"]],
        "b_fc1_1": [l1["ff_b1"]], "ln_w": [l1["ln1_w"], l1["ln2_w"]], "ln_b": [l1["ln1_b"], l1["ln2_b"]],
        "g_b": [l1["g1_b"], l1["g2_b"]], "beta_b": [l1["b1_b"], l1["b2_b"]],
    }
    cols = [feature_columns(x) for name, _ in COLS[:9] for x in vectors[name]]
    cols += [feature_columns(l1["ca_lnc_w"], KC), feature_columns(l1["ca_lnc_b"], KC), mask]
    arrays = {
        "x": v["x"], "ctx": v["ctx_768"],
        "ctxT": v["ctx_768"].reshape(B, M, CC, KC).transpose(0, 3, 2, 1),
        "condT": chunked(v["cond_1024"].T), "cols": np.concatenate(cols, axis=1),
        "rows": np.stack([l0["b_proj"], l0["b_out"], l0["b_fc2"], l1["sa_bo"], l1["ca_bo"], l1["ff_b2"]]).reshape(2, ROWS, D),
        "ident": np.eye(P, dtype=np.float32), "cos": cos, "sin": sin,
        "wada": chunked(l0["W_ada"]),
        "wmod": np.stack([chunked(l1[n]) for n in ("g1_w", "b1_w", "g2_w", "b2_w")], axis=1),
        "wctxT": chunked(l0["W_ctx"].T), "w0_k": chunked(l0["W_k"]), "w0_v": chunked(l0["W_v"]),
        "w0_qkv": chunked(l0["W_qkv"]), "w0_o": chunked(l0["W_proj"]), "w0_cq": chunked(l0["W_q"]),
        "w0_co": chunked(l0["W_out"]), "w0_f1": chunked(l0["W_fc1"]), "w0_f2": chunked(l0["W_fc2"]),
        "w1_q": chunked(rotary_columns(l1["sa_wq"])), "w1_k": chunked(rotary_columns(l1["sa_wkv"][:, :WIDTH[1]])),
        "w1_v": chunked(l1["sa_wkv"][:, WIDTH[1]:]), "w1_o": chunked(l1["sa_wo"]),
        "w1_cq": chunked(rotary_columns(l1["ca_wq"])), "w1_ck": chunked(rotary_columns(l1["ca_wkv"][:, :WIDTH[1]]), KC),
        "w1_cv": chunked(l1["ca_wkv"][:, WIDTH[1]:], KC), "w1_co": chunked(l1["ca_wo"]),
        "w1_f1": chunked(l1["ff_w1"]), "w1_f2": chunked(l1["ff_w2"]),
    }
    nc = bacc.Bacc("TRN2", target_bir_lowering=False, num_devices=1)
    args = {}
    for name in arrays:
        arrays[name] = np.ascontiguousarray(arrays[name])
        args[name] = nc.dram_tensor("in_" + name, arrays[name].shape, F32, kind="ExternalInput").ap()
    out = nc.dram_tensor("out", [B, N, D], F32, kind="ExternalOutput").ap()
    two_blocks(nc, args, out)
    return run_bass_kernel_spmd(nc, [{"in_" + n: x for n, x in arrays.items()}], core_ids=[0]).results[0]["out"]
```

```python
from contextlib import ExitStack

import numpy as np

import concourse.bass as bass
from concourse import mybir

F32, F32R = mybir.dt.float32, mybir.dt.float32r
ALU = mybir.AluOpType
ACT = mybir.ActivationFunctionType
AX_X = mybir.AxisListType.X

P = 128
B, N, D = 32, 100, 256
M, DC = 361, 192
H = 16
FF = 4 * D
PAIR = 2
ROUNDS = B // PAIR
T = PAIR * N
C = D // P
CF = FF // P
KC = 96
CC = DC // KC
MP = 121
MCH = [(m, min(MP, M - m)) for m in range(0, M, MP)]
NM = len(MCH)
HD = [D // H, 64]
WIDTH = [H * d for d in HD]
CW = [w // P for w in WIDTH]
EPS = [1e-6, 1e-5]
SCALE = [d ** -0.5 for d in HD]
SC_BANKS = 3
LAG = 3
SELF_HEADS = 4
BANK = 512
MR = M + M % 2
SPLIT = ((0, 0), (0, 1), (1, 0))
MASKED_PAIRS = 2
MASKED_AHEAD = 4
HEADS_OF = {"self": SELF_HEADS, "cross": 1}
KEYS_OF = {"self": N, "cross": M}
GROUPS_OF = {k: PAIR * H // n for k, n in HEADS_OF.items()}
GROUPS = sum(GROUPS_OF.values())
TOK_PARTS = [1, 2]
TOK_JOBS = [PAIR * (2 * parts + 3) for parts in TOK_PARTS]
NORMS = [3, 4]
ROT = 2
ROTATIONS = (3 + PAIR) * CW[1] // ROT
SWAP = [(p + 16) % 32 for p in range(32)]
KEY_ROTATIONS = PAIR * CW[1] // ROT
KEYS_LATER = 2
CTX_MARKS = 2 * PAIR * NM
MARKS_AHEAD = [2 * PAIR, 2 * PAIR + CTX_MARKS + 3 * (KEY_ROTATIONS - KEYS_LATER)]
VECTOR_MARKS = [3 * 2 * PAIR + PAIR * 2 * TOK_PARTS[0],
                CTX_MARKS + 3 * 2 * PAIR + PAIR * 2 * TOK_PARTS[1] + 3 * ROTATIONS]

FILLS = [
    {"first": 0, "self": {8: 1, 9: 1}, "b2_t": 2, "b2_q": 1, "b2_s": 2, "cross": {1: 1, 32: 1}, "b3_t": 2, "b3_f1": 1, "b3_f2": 0},
    {"first": 6, "self": {1: 1, 8: 1, 9: 1}, "b2_t": 2, "b2_q": 1, "b2_s": 4, "cross": {32: 1, 33: 1}, "b3_t": 3, "b3_f1": 11, "b3_f2": 0},
]
NEXT_ROWS = [(1, 3, 5), (1, 3, 5)]
NEXT_CONTEXT = {"stats": 3, "variance": 3 + PAIR * NM, "norm": 13, "features": 15 + PAIR * NM}

COLS = [("b_ada", 12), ("b_qkv", 6), ("b_ctx", 2), ("b_fc1_0", 8), ("b_fc1_1", 8), ("ln_w", 4), ("ln_b", 4),
        ("g_b", 4), ("beta_b", 4), ("lnc_w", 2), ("lnc_b", 2), ("mask", 8)]
ROWS = 3


def lin_order(L):
    cw, banks = CW[L], TOK_PARTS[L]
    rows = [("next_t", C)] + ([("ctx_t", PAIR * CC)] if L == 1 else [])
    kinds = [("cv", PAIR * NM * banks), ("nv", PAIR * banks), ("nk", PAIR * cw)]
    queue = [(kind, k) for kind, n in kinds for k in range(n)]
    order, places = [], {}

    def fill(place, n):
        places[place] = [queue.pop(0) for _ in range(n)]
        order.extend(places[place])

    def some(name, n):
        order.extend((name, k) for k in range(n))

    f = FILLS[L]
    some("q", cw), some("k", cw), fill("first", f["first"])
    for s in range(GROUPS_OF["self"] + LAG):
        fill(("self", s), f["self"].get(s, 0))
        if s == NEXT_ROWS[L][2]:
            some(*rows[0])
    some("o1", PAIR * banks), fill("b2_t", f["b2_t"]), some("t1", C), fill("b2_q", f["b2_q"]), some("q2", cw)
    fill("b2_s", f["b2_s"])
    assert not [k for k in queue if k[0] == "cv"]
    for s in range(GROUPS_OF["cross"] + LAG):
        fill(("cross", s), f["cross"].get(s, 0))
        if L == 1 and 0 <= s - NEXT_CONTEXT["features"] < PAIR * CC:
            order.append(("ctx_t", s - NEXT_CONTEXT["features"]))
    some("o2", PAIR * banks), fill("b3_t", f["b3_t"]), some("t2", C), fill("b3_f1", f["b3_f1"]), some("f1", CF)
    fill("b3_f2", f["b3_f2"])
    assert not queue
    before = [(name, k) for name, n in rows[0:1] + kinds[1:2] + rows[1:2] + kinds[2:3] for k in range(n)]
    assert len(order) % 2 == 0 and len(before) % 2 == 0
    return {job: n for n, job in enumerate(order)}, len(order), places, {job: n for n, job in enumerate(before)}


class Count:

    def __init__(self, i, per, start=0):
        self.i, self.per, self.start, self.n = i, per, start, 0

    def at(self, n):
        return self.i * self.per + (self.start + n)

    def next(self):
        self.n += 1
        return self.at(self.n)

    def end(self):
        assert self.n == self.per, (self.n, self.per)


def group_heads(kind, g):
    b, h = divmod(g * HEADS_OF[kind], H)
    return b, list(range(h, h + HEADS_OF[kind]))


def spread(ap, shape):
    return ap.rearrange("p (m o) -> p m o", o=1).broadcast_to(shape)


def two_blocks(nc, a, out):
    with ExitStack() as ctx:
        def sb(name, shape):
            return ctx.enter_context(nc.sbuf_tensor(name, list(shape), F32))

        def sem(name):
            return ctx.enter_context(nc.semaphore(name))

        lin, sc, tr, tok = (ctx.enter_context(nc.psum_tensor(n, [P, banks, BANK], F32))
                            for n, banks in (("lin", 2), ("sc", SC_BANKS), ("tr", 1), ("tok", 2)))

        w1 = {n: sb("w1_" + n, a["w1_" + n].shape) for n in ("q", "k", "v", "o", "cq", "co")}
        cols = sb("cols_sb", [P, sum(n for _, n in COLS)])
        ident, rows = sb("ident_sb", [P, P]), sb("rows_sb", [N, ROWS, D])
        cos, sin = sb("cos_sb", [P, M]), sb("sin_sb", [P, M])
        mod1 = sb("mod1", [P, 8, B + PAIR])
        modcur, modnext = sb("modcur", [P, 12, PAIR]), sb("modnext", [P, 2 * C, PAIR])
        derived = sb("derived", [P, 3, C])
        half = sb("half", [P, 2 * NM])
        norm = {n: sb(n, s) for n, s in (("stats", [P, 6, 6]), ("mv", [P, 6, 2]), ("veps", [P, 6]), ("rstd", [P, 6]))}
        soft = {n: sb(n, [N, PAIR, H]) for n in ("negmax", "sums", "rinv")}
        arena = sb("arena", [P, ARENA])
        split_arena = ctx.enter_context(nc.sbuf_tensor("split_arena", [P, SPLIT_ARENA], F32R))
        used = [0]

        def carve(p, *shape):
            n = int(np.prod(shape))
            ap = arena[0:p, used[0]:used[0] + n]
            used[0] += n
            assert used[0] <= ARENA, used[0]
            dims = "abcd"[:len(shape)]
            if len(shape) > 1:
                ap = ap.rearrange(f"p ({' '.join(dims)}) -> p {' '.join(dims)}", **dict(zip(dims, shape)))
            return ap

        def carve_split(start, p, *shape):
            n = 2 * int(np.prod(shape))
            assert start + n <= SPLIT_ARENA
            ap = split_arena[0:p, start:start + n]
            dims = "abcd"[:len(shape) + 1]
            return ap.rearrange(f"p ({' '.join(dims)}) -> p {' '.join(dims)}", **dict(zip(dims, (2,) + shape))), start + n

        at, pos = {}, 0
        for name, n in COLS:
            at[name] = cols[:, pos:pos + n]
            pos += n
        at["bq"], at["b_ck"], at["b_cv"] = derived[:, 0], derived[:, 1], derived[:, 2]

        x_mid = nc.dram_tensor("x_mid", [B, N, D], F32, kind="Internal").ap()
        w1_loaded = sem("w1_loaded")

        w0 = {n: carve(P, *a["w0_" + n].shape[1:]) for n in ("qkv", "o", "cq", "co", "f1", "f2")}
        w0["ck"], w0["cv"] = carve(KC, CC, D), carve(KC, CC, D)
        mods = [carve(P, 12, B + PAIR), mod1]
        layer0_start = used[0]
        setup(nc, sem, carve, a, at, w0, w1, cols, ident, cos, sin, mods, derived, half, lin, sc, tr, w1_loaded)
        used[0] = layer0_start
        layer(nc, 0, sem, carve, carve_split, a, at, w0, a["x"], x_mid, ident, rows, mods[0], modcur, modnext, half, norm, soft,
              lin, sc, tr, tok, cos, sin, w1_loaded)
        used[0] = 0
        layer(nc, 1, sem, carve, carve_split, a, at, w1, x_mid, out, ident, rows, mods[1], modcur, modnext, half, norm, soft,
              lin, sc, tr, tok, cos, sin, w1_loaded)


ARENA = 27600
SPLIT_ARENA = 11088


def setup(nc, sem, carve, a, at, w0, w1, cols, ident, cos, sin, mods, derived, half, lin, sc, tr, w1_loaded):
    wada, wmod = carve(P, C, 12 * P), carve(P, 4, C, D)
    wctxT, wk, wv = carve(P, C, DC), carve(P, C, D), carve(P, C, D)
    condT, silu_c, gain = carve(P, C, B), carve(P, C, B), carve(P, 2, C, B)
    vectors_loaded, factors_loaded, rest_loaded = sem("vectors_loaded"), sem("factors_loaded"), sem("rest_loaded")
    silu_done, folded_out = sem("silu_done"), sem("folded_out")
    mod0_ready, mod1_ready, fold_ready, bias_ready = (sem(n) for n in ("mod0_ready", "mod1_ready", "fold_ready", "bias_ready"))
    step = sem("setup_step")

    with nc.Block() as block:
        @block.sync
        def _(sp):
            sp.dma_start(condT, a["condT"]).then_inc(vectors_loaded, 16)
            sp.dma_start(cols[:], a["cols"]).then_inc(vectors_loaded, 16)
            for dst, name in ((wada, "wada"), (wmod, "wmod"), (wctxT, "wctxT"), (wk, "w0_k"), (wv, "w0_v")):
                sp.dma_start(dst, a[name]).then_inc(factors_loaded, 16)
            loads = [(w0[n], a["w0_" + n]) for n in ("qkv", "o", "cq", "co", "f1", "f2")]
            loads += [(ident[:], a["ident"]), (cos[:], a["cos"]), (sin[:], a["sin"])]
            for dst, src in loads:
                sp.dma_start(dst, src).then_inc(rest_loaded, 16)
            for name, dst in w1.items():
                sp.dma_start(dst[:], a["w1_" + name]).then_inc(w1_loaded, 16)
            sp.wait_ge(rest_loaded, 16 * len(loads))

        @block.scalar
        def _(act):
            act.wait_ge(vectors_loaded, 32)
            nc.scalar.activation(silu_c, condT, ACT.Silu).then_inc(silu_done, 1)
            act.wait_ge(fold_ready, 1)
            for bank, dst in enumerate((w0["ck"], w0["cv"])):
                nc.scalar.copy(dst, sc[0:KC, bank, 0:CC * D].rearrange("p (c n) -> p c n", c=CC)).then_inc(folded_out, 1)
            act.wait_ge(folded_out, 2)

        @block.tensor
        def _(pe):
            pe.wait_ge(silu_done, 1)
            pe.wait_ge(factors_loaded, 80)
            for m in range(12):
                for c in range(C):
                    mm = nc.tensor.matmul(lin[:, 0, m * B:(m + 1) * B], wada[:, c, m * P:(m + 1) * P],
                                          silu_c[:, c, :], start=(c == 0), stop=(c == C - 1))
            mm.then_inc(mod0_ready, 1)
            for k in range(4):
                for m in range(C):
                    o = (k * C + m) * B
                    for c in range(C):
                        mm = nc.tensor.matmul(lin[:, 1, o:o + B], wmod[:, k, c, m * P:(m + 1) * P],
                                              condT[:, c, :], start=(c == 0), stop=(c == C - 1))
            mm.then_inc(mod1_ready, 1)
            for bank, w in enumerate((wk, wv)):
                for r in range(CC):
                    for c in range(C):
                        mm = nc.tensor.matmul(sc[0:KC, bank, r * D:(r + 1) * D], wctxT[:, c, r * KC:(r + 1) * KC],
                                              w[:, c, :], start=(c == 0), stop=(c == C - 1))
            mm.then_inc(fold_ready, 1)
            for j, w in enumerate((wk, wv)):
                for m in range(C):
                    for c in range(C):
                        mm = nc.tensor.matmul(tr[:, 0, C * j + m:C * j + m + 1], w[:, c, m * P:(m + 1) * P],
                                              at["b_ctx"][:, c:c + 1], start=(c == 0), stop=(c == C - 1))
            mm.then_inc(bias_ready, 1)

        @block.vector
        def _(dve):
            done = [0]

            def then_wait(ins):
                done[0] += 1
                ins.then_inc(step, 1)
                dve.wait_ge(step, done[0])

            then_wait(nc.vector.memset(half[:], -0.5))
            for mod in mods:
                then_wait(nc.vector.memset(mod[:, :, B:B + PAIR], 0.0))
            dve.wait_ge(vectors_loaded, 32)
            then_wait(nc.vector.tensor_scalar(derived[:, 0], at["b_qkv"][:, 0:C], SCALE[0], None, ALU.mult))
            dve.wait_ge(mod0_ready, 1)
            then_wait(nc.vector.tensor_tensor(mods[0][:, :, 0:B], lin[:, 0, 0:12 * B].rearrange("p (m b) -> p m b", b=B),
                                              spread(at["b_ada"], [P, 12, B]), ALU.add))
            for s in range(3):
                scale = mods[0][:, 4 * s + C:4 * s + 2 * C, 0:B]
                then_wait(nc.vector.tensor_scalar(scale, scale, 1.0, None, ALU.add))
            dve.wait_ge(mod1_ready, 1)
            for k in range(2):
                g, beta = (lin[:, 1, j * C * B:(j + 1) * C * B].rearrange("p (m b) -> p m b", b=B) for j in (2 * k, 2 * k + 1))
                of = {n: spread(at[n][:, k * C:(k + 1) * C], [P, C, B]) for n in ("g_b", "ln_w", "ln_b", "beta_b")}
                shift, scale = mods[1][:, 4 * k:4 * k + C, 0:B], mods[1][:, 4 * k + C:4 * k + 2 * C, 0:B]
                then_wait(nc.vector.tensor_tensor(gain[:, 0], g, of["g_b"], ALU.add))
                then_wait(nc.vector.tensor_scalar(gain[:, 0], gain[:, 0], 1.0, None, ALU.add))
                then_wait(nc.vector.tensor_tensor(scale, gain[:, 0], of["ln_w"], ALU.mult))
                then_wait(nc.vector.tensor_tensor(gain[:, 1], gain[:, 0], of["ln_b"], ALU.mult))
                then_wait(nc.vector.tensor_tensor(shift, beta, gain[:, 1], ALU.add))
                then_wait(nc.vector.tensor_tensor(shift, shift, of["beta_b"], ALU.add))
            dve.wait_ge(bias_ready, 1)
            then_wait(nc.vector.tensor_copy(derived[:, 1:3], tr[:, 0, 0:2 * C].rearrange("p (j c) -> p j c", c=C)))


def layer(nc, L, sem_of, carve, carve_split, a, at, w, x_src, x_dst, ident, rows, mod, modcur, modnext, half, norm, soft,
          lin, sc, tr, tok, cos, sin, w1_loaded):
    hd, cw, width, parts = HD[L], CW[L], WIDTH[L], TOK_PARTS[L]
    stats, mv, veps, rstd = (norm[n] for n in ("stats", "mv", "veps", "rstd"))
    negmax, sums, rinv = (soft[n] for n in ("negmax", "sums", "rinv"))
    J, LIN, PLACES, J_AHEAD = lin_order(L)
    AHEAD = len(J_AHEAD)
    TOK, MARKS = TOK_JOBS[L], VECTOR_MARKS[L]
    QREADY = cw + H if L == 0 else ROTATIONS
    QAHEAD = 0 if L == 0 else KEY_ROTATIONS - KEYS_LATER
    Q2FIRST = 2 * cw // ROT + KEYS_LATER + 1
    part_heads = H // parts
    part_cols = width // parts
    part_chunks = cw // parts
    w_q = w["qkv"][:, :, 0:D] if L == 0 else w["q"]
    w_k = w["qkv"][:, :, D:2 * D] if L == 0 else w["k"]
    w_v = w["qkv"][:, :, 2 * D:3 * D] if L == 0 else w["v"]
    ctx_values = [(b, t, h) for b in range(PAIR) for t in range(NM) for h in range(parts)]
    own_values = [(b, h) for b in range(PAIR) for h in range(parts)]
    key_chunks = [(b, m) for b in range(PAIR) for m in range(cw)]

    def sem(name):
        return sem_of(f"{name}_{L}")

    x_in = carve(N, PAIR, D)
    x_now = carve(N, PAIR, D)
    xn = carve(N, PAIR, D)
    hT = carve(P, C, T)
    hT0 = carve(P, C, T)
    qT, kT = carve(P, cw, T), carve(P, cw, T)
    qmask = carve(P, cw, P // hd, T)
    v_self = carve(N, PAIR, width)
    kc = carve(P, PAIR, cw, M)
    vc_room = carve(P, PAIR * NM * width)
    vc = vc_room[0:MP].rearrange("p (b t n) -> p b t n", b=PAIR, t=NM)
    if L == 0:
        ctxT = carve(KC, PAIR, CC, M)
        q_split, end = carve_split(0, P, cw, P // hd, T)
        k_split, _ = carve_split(end, P, PAIR, cw, MR)
    else:
        ctx_split, end = carve_split(0, KC, PAIR, CC, MR)
        ck_split, end = carve_split(end, KC, CC, width)
        cv_split, _ = carve_split(end, KC, CC, width)
    prob = carve(N, SC_BANKS, 400)
    shared = carve(P, 2 * 400)
    probT = shared[0:MP].rearrange("p (two n) -> p two n", two=2)
    o_tok = carve(N, PAIR, width)
    oT = kT
    if L == 0:
        gT = carve(P, CF, T)
    else:
        gT = qT
        ctx_in = kT.rearrange("p c t -> p (c t)")[0:MP, 0:PAIR * NM * DC].rearrange("p (t d) -> p t d", d=DC)
        loads_w1 = len(w)
        ck_whole, cv_whole = (vc_room[0:KC, n:n + CC * width].rearrange("p (c n) -> p c n", c=CC) for n in (0, CC * width))
        ctx_whole = hT.rearrange("p c t -> p (c t)")[0:KC, 0:M]
        w = dict(w, f1=vc_room[:, 0:C * FF].rearrange("p (c n) -> p c n", c=C),
                 f2=vc_room[:, C * FF:C * FF + CF * D].rearrange("p (c n) -> p c n", c=CF))
        swapped = shared

    x_loaded, ctx_loaded, x_stored, rows_loaded = (sem(n) for n in ("x_loaded", "ctx_loaded", "x_stored", "rows_loaded"))
    x_in_free, ctx_free = sem("x_in_free"), sem("ctx_free")
    cross_done, mlp_loaded = sem("cross_done"), sem("mlp_loaded")
    halves_ready = sem("halves_ready")
    q_masked = sem("q_masked")
    high_ready = sem("high_ready")
    raw_loaded, raw_high, raw_split = sem("raw_loaded"), sem("raw_high"), sem("raw_split")
    ctx_rows = sem("ctx_rows")
    lin_ready, lin_out = sem("lin_ready"), sem("lin_out")
    tok_ready, tok_out = sem("tok_ready"), sem("tok_out")
    sc_ready, max_ready, prob_ready = sem("sc_ready"), sem("max_ready"), sem("prob_ready")
    tr_ready, probT_ready = sem("tr_ready"), sem("probT_ready")
    var_ready, rstd_ready, xn_ready = sem("var_ready"), sem("rstd_ready"), sem("xn_ready")
    bias_added, mod_ready = sem("bias_added"), sem("mod_ready")
    q_ready = sem("q_ready")
    cleared, step, stats_seen = sem("cleared"), sem("vector_step"), sem("stats_seen")
    ctx_dmas = PAIR if L == 0 else 2 * PAIR

    with nc.Block() as block:
        @block.sync
        def _(sp):
            def load_x(pair):
                sp.dma_start(x_in, x_src[bass.ds(pair * PAIR, PAIR)].rearrange("b n d -> n b d")).then_inc(x_loaded, 16)

            def load_context(pair):
                for b in range(PAIR):
                    if L == 0:
                        sp.dma_start(ctxT[:, b], a["ctxT"][bass.ds(pair * PAIR + b, 1)].rearrange("o p c m -> (o p) c m"))\
                          .then_inc(ctx_loaded, 16)
                    else:
                        src = a["ctx"][bass.ds(pair * PAIR + b, 1)].rearrange("o m d -> (o m) d")
                        whole, rest = MCH[-1]
                        sp.dma_start(ctx_in[:, b * NM:b * NM + NM - 1, :],
                                     src[0:whole].rearrange("(t p) d -> p t d", p=MP)).then_inc(ctx_loaded, 16)
                        sp.dma_start(ctx_in[0:rest, b * NM + NM - 1, :], src[whole:M]).then_inc(ctx_loaded, 16)

            def load_mlp(round_):
                if L == 1:
                    sp.wait_ge(cross_done, round_ + 1)
                    for name in ("f1", "f2"):
                        sp.dma_start(w[name], a["w1_" + name]).then_inc(mlp_loaded, 16)

            def store(pair):
                sp.wait_ge(tok_out, pair * TOK + (2 + TOK))
                sp.dma_start(x_dst[bass.ds(pair * PAIR, PAIR)].rearrange("b n d -> n b d"), x_now).then_inc(x_stored, 16)

            sp.sem_inc(x_stored, 16)
            load_x(0)
            sp.dma_start(rows[:], a["rows"][L].partition_broadcast(N)).then_inc(rows_loaded, 16)
            if L == 1:
                for dst, name in ((ck_whole, "ck"), (cv_whole, "cv")):
                    sp.dma_start(dst, a["w1_" + name]).then_inc(raw_loaded, 16)
                sp.wait_ge(cleared, 1)
            load_context(0)
            with nc.Fori(0, ROUNDS - 1, engines=[sp.engine]) as i:
                sp.wait_ge(x_in_free, i + 1)
                load_x(i + 1)
                sp.wait_ge(ctx_free, i + 1)
                load_context(i + 1)
                load_mlp(i)
                store(i)
            sp.wait_ge(x_in_free, ROUNDS)
            load_x(0)
            sp.wait_ge(ctx_free, ROUNDS)
            load_context(0)
            load_mlp(ROUNDS - 1)
            store(ROUNDS - 1)
            sp.wait_ge(x_stored, 16 * (ROUNDS + 1))

        @block.gpsimd
        def _(pool):
            def inverse_root(value, p, n):
                pool.wait_ge(var_ready, value)
                nc.gpsimd.tensor_tensor(rstd[0:p, 0:n], veps[0:p, 0:n], half[0:p, 0:n], ALU.pow).then_inc(rstd_ready, 1)

            nc.gpsimd.tensor_copy(modnext[:], mod[:, 0:2 * C, 0:PAIR]).then_inc(mod_ready, 1)
            inverse_root(1, N, PAIR)
            if L == 1:
                inverse_root(2, MP, PAIR * NM)
            pool.wait_ge(rows_loaded, 16)
            with nc.Fori(0, ROUNDS, engines=[pool.engine]) as i:
                roots = Count(i, NORMS[L], 1 + L)
                pool.wait_ge(lin_out, i * LIN + (2 + AHEAD))
                n_mod = mod.shape[1]
                nc.gpsimd.tensor_copy(modcur[:, 0:n_mod, :], mod[:, :, bass.ds(i * PAIR, PAIR)])
                nc.gpsimd.tensor_copy(modnext[:], mod[:, 0:2 * C, bass.ds(i * PAIR + PAIR, PAIR)]).then_inc(mod_ready, 1)

                def add_bias(src, r):
                    nc.gpsimd.tensor_tensor(x_now, src, rows[:, r:r + 1, :].broadcast_to([N, PAIR, D]), ALU.add)\
                      .then_inc(bias_added, 1)

                pool.wait_ge(x_loaded, i * 16 + 16)
                pool.wait_ge(x_stored, i * 16 + 16)
                add_bias(x_in, 0)
                pool.wait_ge(xn_ready, i * 6 + 2)
                pool.wait_ge(bias_added, i * 3 + 1)
                pool.sem_inc(x_in_free, 1)
                inverse_root(roots.next(), N, PAIR)
                inverse_root(roots.next(), N, PAIR)
                pool.wait_ge(xn_ready, i * 6 + 6)
                add_bias(x_now, 1)
                if L == 1:
                    inverse_root(roots.next(), MP, PAIR * NM)
                inverse_root(roots.next(), N, PAIR)
                pool.wait_ge(xn_ready, i * 6 + 8)
                add_bias(x_now, 2)
                roots.end()

        @block.scalar
        def _(act):
            act.sem_inc(lin_out, 2)

            def bank_of(n, value):
                act.wait_ge(lin_ready, value)
                return lin[:, n % 2]

            def evict_modulated(take, dst, mods, s):
                for c in range(C):
                    ps = take()
                    for b in range(PAIR):
                        ins = nc.scalar.activation(dst[:, c, b * N:(b + 1) * N], ps[:, b * N:(b + 1) * N], ACT.Identity,
                                                   bias=mods[:, s + c, b:b + 1], scale=mods[:, s + C + c, b:b + 1])
                    ins.then_inc(lin_out, 1)

            def evict_context(take, k, before):
                b, c = divmod(k, CC)
                ps = take()
                if before is not None:
                    act.wait_ge(halves_ready, before)
                for dst in (ctx_whole, ctx_split[:, 0, b, c, 0:M]):
                    ins = nc.scalar.activation(dst, ps[0:KC, 0:M], ACT.Identity, bias=at["lnc_b"][0:KC, c:c + 1],
                                               scale=at["lnc_w"][0:KC, c:c + 1])
                ins.then_inc(lin_out, 1)

            def evict_fills(take, jobs):
                for kind, k in jobs:
                    ps = take()
                    if kind == "cv":
                        b, t, h = ctx_values[k]
                        mn = MCH[t][1]
                        ins = nc.scalar.copy(vc[0:mn, b, t, h * part_cols:(h + 1) * part_cols], ps[0:mn, 0:part_cols])
                    elif kind == "nv":
                        b, h = own_values[k]
                        ins = nc.scalar.copy(v_self[:, b, h * part_cols:(h + 1) * part_cols], ps[0:N, 0:part_cols])
                    else:
                        b, m = key_chunks[k]
                        if L == 0:
                            for dst in (kc[:, b, m, :], k_split[:, 0, b, m, 0:M]):
                                ins = nc.scalar.activation(dst, ps[:, 0:M], ACT.Identity, bias=at["b_ck"][:, m:m + 1])
                        else:
                            ins = nc.scalar.copy(kc[:, b, m, :], ps[:, 0:M])
                    ins.then_inc(lin_out, 1)

            ahead = [0]

            def take_ahead():
                ahead[0] += 1
                return bank_of(ahead[0] - 1, ahead[0])

            if L == 1:
                act.wait_ge(raw_loaded, 32)
                for dst, whole in ((ck_split, ck_whole), (cv_split, cv_whole)):
                    nc.scalar.copy(dst[:, 0], whole).then_inc(raw_high, 1)

            act.wait_ge(mod_ready, 1)
            evict_modulated(take_ahead, hT0, modnext, 0)
            evict_fills(take_ahead, [job for job in J_AHEAD if job[0] == "nv"])
            if L == 1:
                for k in range(PAIR * CC):
                    evict_context(take_ahead, k, k if k else None)
            evict_fills(take_ahead, [job for job in J_AHEAD if job[0] == "nk"])
            assert ahead[0] == AHEAD

            with nc.Fori(0, ROUNDS, engines=[act.engine]) as i:
                filled = Count(i, LIN, AHEAD)
                maxima = Count(i, GROUPS)

                def take():
                    n = filled.n
                    return bank_of(n, filled.next())

                def evict_chunks(dst, n, scale, bias=None):
                    for c in range(cw):
                        ps = take()
                        if bias is None:
                            nc.scalar.activation(dst[:, c, :], ps[:, 0:n], ACT.Copy, scale=scale).then_inc(lin_out, 1)
                        else:
                            nc.scalar.activation(dst[:, c, :], ps[:, 0:n], ACT.Identity, scale=scale,
                                                 bias=bias[:, c:c + 1]).then_inc(lin_out, 1)

                def probabilities(kind, beside={}):
                    keys = KEYS_OF[kind]
                    for g in range(GROUPS_OF[kind] + LAG):
                        if g < GROUPS_OF[kind]:
                            n = maxima.n
                            b, hs = group_heads(kind, g)
                            act.wait_ge(max_ready, maxima.next())
                            for k, h in enumerate(hs):
                                ins = nc.scalar.activation(prob[:, n % SC_BANKS, k * keys:(k + 1) * keys],
                                                           sc[0:N, n % SC_BANKS, k * keys:(k + 1) * keys], ACT.Exp,
                                                           bias=negmax[:, b, h:h + 1], accum_out=sums[:, b, h:h + 1])
                            ins.then_inc(prob_ready, 1)
                        evict_fills(take, PLACES[kind, g])
                        if g in beside:
                            beside[g]()

                def mask_rotated(k, value):
                    act.wait_ge(q_ready, i * QREADY + (QAHEAD + value))
                    c = k * ROT
                    for j in range(P // hd):
                        rows_ = slice(j * hd, (j + 1) * hd)
                        ins = nc.scalar.copy(qmask[rows_, c:c + ROT, j, :], qT[rows_, c:c + ROT, :])
                    ins.then_inc(q_masked, 1)

                def fills_and_masks(jobs, masks, value):
                    k = 0
                    for n, job in enumerate(jobs):
                        evict_fills(take, [job])
                        while k < masks and (k + 1) * len(jobs) <= (n + 1) * masks:
                            mask_rotated(k, value + k)
                            k += 1

                def evict_attention(bias):
                    for b in range(PAIR):
                        for h in range(parts):
                            ps = take()[:, 0:part_chunks * N].rearrange("p (c n) -> p c n", n=N)
                            dst = oT[:, h * part_chunks:(h + 1) * part_chunks, b * N:(b + 1) * N]
                            if bias is None:
                                ins = nc.scalar.copy(dst, ps)
                            else:
                                for c in range(part_chunks):
                                    ins = nc.scalar.activation(dst[:, c], ps[:, c], ACT.Identity, bias=bias[:, c:c + 1])
                            ins.then_inc(lin_out, 1)

                evict_chunks(qT, T, SCALE[L], at["bq"] if L == 0 else None)
                evict_chunks(kT, T, 1.0, at["b_qkv"][:, C:2 * C] if L == 0 else None)
                if L == 1:
                    fills_and_masks(PLACES["first"], cw // ROT, 1)
                else:
                    evict_fills(take, PLACES["first"])
                act.wait_ge(mod_ready, i + 2)
                probabilities("self", {NEXT_ROWS[L][2]: lambda: evict_modulated(take, hT0, modnext, 0)})
                evict_attention(at["b_qkv"][:, 2 * C:3 * C] if L == 0 else None)
                evict_fills(take, PLACES["b2_t"])
                evict_modulated(take, hT, modcur, 2 * C if L == 0 else 0)
                evict_fills(take, PLACES["b2_q"])
                evict_chunks(qT, T, SCALE[L])
                if L == 0:
                    def high_queries(h):
                        c, j = divmod(h, P // hd)
                        if h in (0, MASKED_AHEAD):
                            act.wait_ge(lin_out, i * LIN + (2 + AHEAD + J["q2", cw - 1 if h else 0] + 1))
                        nc.scalar.activation(q_split[:, 0, c, j, :], qT[:, c, :], ACT.Copy, scale=at["mask"][:, j:j + 1])\
                          .then_inc(high_ready, 1)

                    for h in range(MASKED_AHEAD):
                        high_queries(h)
                if L == 1:
                    fills_and_masks(PLACES["b2_s"], MASKED_PAIRS, Q2FIRST)
                else:
                    evict_fills(take, PLACES["b2_s"])
                if L == 0:
                    beside = {s: lambda h=s + MASKED_AHEAD: high_queries(h) for s in range(H - MASKED_AHEAD)}
                else:
                    beside = {NEXT_CONTEXT["features"] + k:
                              lambda k=k: evict_context(take, k, i * (PAIR * CC) + (PAIR * CC + k)) for k in range(PAIR * CC)}
                    for k in range(MASKED_PAIRS, cw // ROT):
                        beside[2 * (k - MASKED_PAIRS)] = lambda k=k: mask_rotated(k, Q2FIRST + k)
                probabilities("cross", beside)
                evict_attention(at["b_cv"] if L == 0 else None)
                evict_fills(take, PLACES["b3_t"])
                evict_modulated(take, hT, modcur, 4 * C if L == 0 else 2 * C)
                evict_fills(take, PLACES["b3_f1"])
                for m in range(CF):
                    ps = take()
                    nc.scalar.activation(gT[:, m, :], ps[:, 0:T], ACT.Gelu_apprx_tanh if L == 0 else ACT.Gelu,
                                         bias=at[f"b_fc1_{L}"][:, m:m + 1]).then_inc(lin_out, 1)
                evict_fills(take, PLACES["b3_f2"])
                filled.end()
                maxima.end()

        @block.vector
        def _(dve):
            if L == 1:
                nc.vector.memset(ctx_in, 0.0)
                nc.vector.memset(qmask, 0.0)
                pads = [ctx_split[:, half_, b, :, M:MR] for half_ in range(2) for b in range(PAIR)]
            else:
                pads = [k_split[:, half_, b, :, M:MR] for half_ in range(2) for b in range(PAIR)]
            for pad in pads:
                nc.vector.tensor_scalar(pad, spread(at["mask"][0:pad.shape[0], 0:pad.shape[1]], pad.shape), 0.0, None, ALU.mult)
            nc.vector.memset(tr[:], 0.0).then_inc(cleared, 1)
            dve.sem_inc(tok_out, 2)

            def variance(mark, src, p, n):
                first = [mark(nc.vector.bn_stats(stats[0:p, s, :], src[:, s])) for s in range(n)]
                aggregated(mark, first[-1], p, n)

            def aggregated(mark, stats_there, p, n):
                dve.wait_ge(step, stats_there)
                dve.sem_inc(stats_seen, 1)
                for s in range(n):
                    last = mark(nc.vector.bn_aggr(mv[0:p, s, :], stats[0:p, s, :]))
                dve.wait_ge(step, last)
                nc.vector.tensor_scalar(veps[0:p, 0:n], mv[0:p, 0:n, 1], EPS[L], None, ALU.add).then_inc(var_ready, 1)

            def normalise_tile(s, src, dst, p):
                return nc.vector.tensor_scalar(dst[:, s], src[:, s], mv[0:p, s, 0:1], rstd[0:p, s:s + 1],
                                               ALU.subtract, ALU.mult)

            def normalised(value, src, dst, p, n, done):
                dve.wait_ge(rstd_ready, value)
                for s in range(n):
                    done(normalise_tile(s, src, dst, p))

            marked = [0]

            def mark_ahead(ins):
                marked[0] += 1
                ins.then_inc(step, 1)
                return marked[0]

            def rotate(marked_by, value, after, chunk0, n, reps):
                def runs(ap):
                    return ap.rearrange("p (r n) -> p r n", n=n)

                def table(t):
                    return t[:, 0:n].unsqueeze(1).broadcast_to([P, reps, n])

                buf = chunk0.rearrange("p c t -> p (c t)")
                sw = swapped[:, 0:reps * n]
                dve.wait_ge(lin_out, after)
                by_sin = marked_by(nc.vector.tensor_tensor(runs(sw), runs(buf), table(sin), ALU.mult))
                dve.wait_ge(step, by_sin)
                marked_by(nc.vector.tensor_tensor(runs(buf), runs(buf), table(cos), ALU.mult))
                shuffled = marked_by(nc.vector.stream_shuffle(sw, sw, SWAP))
                dve.wait_ge(step, shuffled)
                nc.vector.tensor_tensor(buf, buf, sw, ALU.add).then_inc(q_ready, 1)
                dve.wait_ge(q_ready, value)

            def rotate_context_keys(marked_by, value_of, after_of, first, end):
                for k in range(first * ROT, end * ROT, ROT):
                    b, m = key_chunks[k]
                    rotate(marked_by, value_of(), after_of(k + ROT - 1), kc[:, b, m:m + ROT, :], M, ROT)

            def split_context(k, after):
                dve.wait_ge(lin_out, after)
                b, c = divmod(k, CC)
                nc.vector.tensor_tensor(ctx_split[:, 1, b, c, 0:M], ctx_whole, ctx_split[:, 0, b, c, 0:M], ALU.subtract)\
                  .then_inc(halves_ready, 1)

            def split_keys(k, after):
                dve.wait_ge(lin_out, after)
                b, m = key_chunks[k]
                nc.vector.tensor_tensor(k_split[:, 1, b, m, 0:M], kc[:, b, m, :], k_split[:, 0, b, m, 0:M], ALU.subtract)\
                  .then_inc(halves_ready, 1)

            dve.wait_ge(x_loaded, 16)
            variance(mark_ahead, x_in, N, PAIR)
            normalised(1, x_in, xn, N, PAIR, lambda ins: ins.then_inc(xn_ready, 1))
            if L == 1:
                rotated = [0]

                def rotated_next():
                    rotated[0] += 1
                    return rotated[0]

                dve.wait_ge(ctx_loaded, 16 * ctx_dmas)
                variance(mark_ahead, ctx_in, MP, PAIR * NM)
                normalised(2, ctx_in, ctx_in, MP, PAIR * NM, lambda ins: ins.then_inc(ctx_rows, 1))
                for n, (dst, whole) in enumerate(((ck_split, ck_whole), (cv_split, cv_whole))):
                    dve.wait_ge(raw_high, n + 1)
                    nc.vector.tensor_tensor(dst[:, 1], whole, dst[:, 0], ALU.subtract).then_inc(raw_split, 1)
                for k in range(PAIR * CC):
                    split_context(k, 2 + J_AHEAD["ctx_t", k] + 1)
                rotate_context_keys(mark_ahead, rotated_next, lambda k: 2 + J_AHEAD["nk", k] + 1,
                                    0, KEY_ROTATIONS - KEYS_LATER)
            else:
                for k in range(PAIR * cw):
                    split_keys(k, 2 + J_AHEAD["nk", k] + 1)
            assert marked[0] == MARKS_AHEAD[L]

            with nc.Fori(0, ROUNDS, engines=[dve.engine]) as i:
                marks = Count(i, MARKS, MARKS_AHEAD[L])
                toks = Count(i, TOK)
                groups = Count(i, GROUPS)
                roots = Count(i, NORMS[L], 1 + L)
                chunks = Count(i, QREADY, QAHEAD)

                def mark(ins):
                    ins.then_inc(step, 1)
                    return marks.next()

                def evicted(*job):
                    return i * LIN + (2 + AHEAD + J[job] + 1)

                def rows_normalised(src):
                    normalised(roots.next(), src, xn, N, PAIR, lambda ins: ins.then_inc(xn_ready, 1))

                def mask_queries(name):
                    for c in range(cw):
                        dve.wait_ge(lin_out, evicted(name, c))
                        nc.vector.tensor_tensor(qmask[:, c], qT[:, c:c + 1, :].broadcast_to([P, P // hd, T]),
                                                spread(at["mask"], [P, P // hd, T]), ALU.mult).then_inc(q_ready, 1)
                        chunks.next()

                def rotate_tokens(src, name, c):
                    rotate(mark, chunks.next(), evicted(name, c + ROT - 1), src[:, c:c + ROT, :], N, ROT * PAIR)

                def attend(kind, beside={}):
                    heads, keys, total = HEADS_OF[kind], KEYS_OF[kind], GROUPS_OF[kind]
                    g0 = groups.n
                    part_groups = part_heads // heads
                    for s in range(total + LAG + 1):
                        if s < total:
                            n = g0 + s
                            b, hs = group_heads(kind, s)
                            dve.wait_ge(sc_ready, groups.next())
                            nc.vector.tensor_reduce(negmax[:, b, hs[0]:hs[-1] + 1],
                                                    sc[0:N, n % SC_BANKS, 0:heads * keys].rearrange("p (h k) -> p h k", h=heads),
                                                    AX_X, ALU.max, negate=True).then_inc(max_ready, 1)
                        if 2 <= s <= total + 1:
                            n = g0 + s - 2
                            p, used = (N, heads * N) if kind == "self" else (MP, NM * N)
                            dve.wait_ge(tr_ready, groups.at(n + 1))
                            nc.vector.tensor_copy(probT[0:p, n % 2, 0:used], tr[0:p, 0, 0:used]).then_inc(probT_ready, 1)
                        if s > LAG and (s - LAG) % part_groups == 0:
                            b, part = divmod((s - LAG) // part_groups - 1, parts)
                            hs = slice(part * part_heads, (part + 1) * part_heads)
                            bank = toks.n % 2
                            dve.wait_ge(tok_ready, toks.next())
                            inverted = mark(nc.vector.reciprocal(rinv[:, b, hs], sums[:, b, hs]))
                            dve.wait_ge(step, inverted)
                            nc.vector.tensor_tensor(
                                o_tok[:, b, part * part_cols:(part + 1) * part_cols].rearrange("p (h d) -> p h d", d=hd),
                                tok[0:N, bank, 0:part_cols].rearrange("p (h d) -> p h d", d=hd),
                                spread(rinv[:, b, hs], [N, part_heads, hd]), ALU.mult).then_inc(tok_out, 1)
                        if s in beside:
                            beside[s]()

                def add_residual(stage):
                    dve.wait_ge(bias_added, i * 3 + (stage + 1))
                    for b in range(PAIR):
                        bank = toks.n % 2
                        dve.wait_ge(tok_ready, toks.next())
                        nc.vector.tensor_tensor(x_now[:, b], tok[0:N, bank, 0:D], x_now[:, b], ALU.add).then_inc(tok_out, 1)
                    dve.wait_ge(tok_out, toks.at(toks.n + 2))

                def next_variance():
                    dve.wait_ge(x_loaded, i * 16 + 32)
                    variance(mark, x_in, N, PAIR)

                def next_context():
                    at_slot = {}
                    for t in range(PAIR * NM):
                        def tile_stats(t=t):
                            if t == 0:
                                dve.wait_ge(ctx_loaded, i * (16 * ctx_dmas) + 32 * ctx_dmas)
                            stats_at.append(mark(nc.vector.bn_stats(stats[0:MP, t, :], ctx_in[:, t])))

                        def tile_normalised(t=t):
                            if t == 0:
                                dve.wait_ge(rstd_ready, roots.next())
                            normalise_tile(t, ctx_in, ctx_in, MP).then_inc(ctx_rows, 1)

                        at_slot[NEXT_CONTEXT["stats"] + t] = tile_stats
                        at_slot[NEXT_CONTEXT["norm"] + t] = tile_normalised
                    stats_at = []
                    for k in range(PAIR * CC):
                        at_slot[NEXT_CONTEXT["features"] + k + 1] = lambda k=k: split_context(k, evicted("ctx_t", k))
                    at_slot[NEXT_CONTEXT["variance"]] = lambda: aggregated(mark, stats_at[-1], MP, PAIR * NM)
                    return at_slot

                if L == 0:
                    mask_queries("q")
                else:
                    for c in range(0, cw, ROT):
                        rotate_tokens(qT, "q", c)
                    for c in range(0, cw, ROT):
                        rotate_tokens(kT, "k", c)
                attend("self", {NEXT_ROWS[L][0]: next_variance, NEXT_ROWS[L][1]: lambda: rows_normalised(x_in)})
                if L == 1:
                    rotate_context_keys(mark, chunks.next, lambda k: i * LIN + (2 + AHEAD),
                                        KEY_ROTATIONS - KEYS_LATER, KEY_ROTATIONS)
                add_residual(0)
                variance(mark, x_now, N, PAIR)
                rows_normalised(x_now)
                if L == 0:
                    def low_queries(h):
                        c, j = divmod(h, P // hd)
                        dve.wait_ge(high_ready, i * H + (h + 1))
                        nc.vector.scalar_tensor_tensor(q_split[:, 1, c, j, :], qT[:, c, :], at["mask"][:, j:j + 1],
                                                       q_split[:, 0, c, j, :], ALU.mult, ALU.subtract).then_inc(q_ready, 1)
                        chunks.next()

                    for h in range(MASKED_AHEAD):
                        low_queries(h)
                    attend("cross", {s + 1: lambda h=s + MASKED_AHEAD: low_queries(h) for s in range(H - MASKED_AHEAD)})
                else:
                    for c in range(0, cw, ROT):
                        rotate_tokens(qT, "q2", c)
                    attend("cross", next_context())
                add_residual(1)
                variance(mark, x_now, N, PAIR)
                rows_normalised(x_now)
                if L == 1:
                    rotate_context_keys(mark, chunks.next, lambda k: evicted("nk", k), 0, KEY_ROTATIONS - KEYS_LATER)
                else:
                    for k in range(PAIR * cw):
                        split_keys(k, evicted("nk", k))
                add_residual(2)
                for count in (marks, toks, groups, roots, chunks):
                    count.end()

        @block.tensor
        def _(pe):
            if L == 1:
                pe.wait_ge(w1_loaded, 16 * loads_w1)
            pe.wait_ge(cleared, 1)

            def bank_of(n, value):
                pe.wait_ge(lin_out, value)
                return lin[:, n % 2]

            def normalised_to_features(take, first):
                for c in range(C):
                    ps = take()
                    for b in range(PAIR):
                        if c == 0:
                            pe.wait_ge(xn_ready, first + b)
                        mm = nc.tensor.transpose(ps[:, b * N:(b + 1) * N], xn[:, b, c * P:(c + 1) * P], ident[0:N, 0:N])
                    mm.then_inc(lin_ready, 1)

            def context_to_features(take, k, value):
                b, c = divmod(k, CC)
                ps = take()
                pe.wait_ge(ctx_rows, value)
                for t, (m0, mn) in enumerate(MCH):
                    mm = nc.tensor.transpose(ps[0:KC, m0:m0 + mn], ctx_in[0:mn, b * NM + t, c * KC:(c + 1) * KC],
                                             ident[0:mn, 0:mn])
                mm.then_inc(lin_ready, 1)

            def accumulate(out, pairs):
                for n, (stationary, moving) in enumerate(pairs):
                    mm = nc.tensor.matmul(out, stationary, moving, start=(n == 0), stop=(n == len(pairs) - 1))
                return mm

            def fill(take, jobs):
                for kind, k in jobs:
                    ps = take()
                    if kind == "cv":
                        b, t, h = ctx_values[k]
                        m0, mn = MCH[t]
                        out, columns = ps[0:mn, 0:part_cols], slice(h * part_cols, (h + 1) * part_cols)
                        if L == 0:
                            pairs = [(ctxT[:, b, c, m0:m0 + mn], w["cv"][:, c, columns]) for c in range(CC)]
                        else:
                            pairs = [(ctx_split[:, x, b, c, m0:m0 + mn], cv_split[:, y, c, columns])
                                     for c in range(CC) for x, y in SPLIT]
                        mm = accumulate(out, pairs)
                    elif kind == "nv":
                        b, h = own_values[k]
                        for c in range(C):
                            mm = nc.tensor.matmul(ps[0:N, 0:part_cols], hT0[:, c, b * N:(b + 1) * N],
                                                  w_v[:, c, h * part_cols:(h + 1) * part_cols],
                                                  start=(c == 0), stop=(c == C - 1))
                    else:
                        b, m = key_chunks[k]
                        columns = slice(m * P, (m + 1) * P)
                        if L == 0:
                            mm = accumulate(ps[:, 0:M], [(w["ck"][:, c, columns], ctxT[:, b, c, :]) for c in range(CC)])
                        else:
                            mm = accumulate(ps[:, 0:MR], [(ck_split[:, x, c, columns], ctx_split[:, y, b, c, :])
                                                          for c in range(CC) for x, y in SPLIT])
                    mm.then_inc(lin_ready, 1)

            ahead = [0]

            def take_ahead():
                ahead[0] += 1
                return bank_of(ahead[0] - 1, ahead[0])

            normalised_to_features(take_ahead, 1)
            pe.wait_ge(lin_out, 2 + C)
            fill(take_ahead, [job for job in J_AHEAD if job[0] == "nv"])
            if L == 1:
                for k in range(PAIR * CC):
                    context_to_features(take_ahead, k, PAIR * NM)
                pe.wait_ge(raw_split, 2)
                pe.wait_ge(halves_ready, PAIR * CC)
            else:
                pe.wait_ge(ctx_loaded, 16 * ctx_dmas)
            fill(take_ahead, [job for job in J_AHEAD if job[0] == "nk"])

            with nc.Fori(0, ROUNDS, engines=[pe.engine], hint_back_edge=True) as i:
                jobs = Count(i, LIN, AHEAD)
                toks = Count(i, TOK)
                groups = Count(i, GROUPS)

                def take():
                    n = jobs.n
                    return bank_of(n, jobs.next())

                def free_tok():
                    n = toks.n
                    pe.wait_ge(tok_out, toks.next())
                    return tok[:, n % 2]

                def evicted(*job):
                    pe.wait_ge(lin_out, i * LIN + (2 + AHEAD + J[job] + 1))

                def project(wt, m, src, n, chunks):
                    ps = take()
                    for c in range(chunks):
                        mm = nc.tensor.matmul(ps[:, 0:n], wt[:, c, m * P:(m + 1) * P], src[:, c, :],
                                              start=(c == 0), stop=(c == chunks - 1))
                    mm.then_inc(lin_ready, 1)

                def attend(kind, beside={}):
                    heads, keys, total = HEADS_OF[kind], KEYS_OF[kind], GROUPS_OF[kind]
                    g0 = groups.n
                    part_groups = part_heads // heads
                    for s in range(total + LAG):
                        if s < total:
                            n = g0 + s
                            b, hs = group_heads(kind, s)
                            if L == 1 and b == 0:
                                pair = hs[-1] * hd // (ROT * P)
                                if kind == "self":
                                    pe.wait_ge(q_ready, i * QREADY + (QAHEAD + cw // ROT + pair + 1))
                                elif pair >= MASKED_PAIRS:
                                    pe.wait_ge(q_masked, i * (2 * cw // ROT) + (cw // ROT + pair + 1))
                            for k, h in enumerate(hs):
                                c, j = divmod(h, P // hd)
                                tokens = slice(b * N, (b + 1) * N)
                                if L == 0 and kind == "cross":
                                    if b == 0:
                                        pe.wait_ge(q_ready, i * QREADY + (cw + h + 1))
                                    mm = accumulate(sc[0:N, n % SC_BANKS, 0:MR],
                                                    [(q_split[:, x, c, j, tokens], k_split[:, y, b, c, :]) for x, y in SPLIT])
                                    continue
                                mm = nc.tensor.matmul(sc[0:N, n % SC_BANKS, k * keys:(k + 1) * keys], qmask[:, c, j, tokens],
                                                      kT[:, c, tokens] if kind == "self" else kc[:, b, c, :],
                                                      start=True, stop=True)
                            mm.then_inc(sc_ready, 1)
                            groups.next()
                        fill(take, PLACES[kind, s])
                        if s in beside:
                            beside[s]()
                        if 2 <= s <= total + 1:
                            n = g0 + s - 2
                            pe.wait_ge(prob_ready, groups.at(n + 1))
                            if s > 2:
                                pe.wait_ge(probT_ready, groups.at(n))
                            tiles = [(k * N, N) for k in range(heads)] if kind == "self" else MCH
                            for t, (m0, mn) in enumerate(tiles):
                                mm = nc.tensor.transpose(tr[0:mn, 0, t * N:(t + 1) * N], prob[:, n % SC_BANKS, m0:m0 + mn],
                                                         ident[0:N, 0:N])
                            mm.then_inc(tr_ready, 1)
                        if s >= LAG:
                            g = s - LAG
                            n = g0 + g
                            b, hs = group_heads(kind, g)
                            if g % part_groups == 0:
                                ps = free_tok()
                            pe.wait_ge(probT_ready, groups.at(n + 1))
                            for k, h in enumerate(hs):
                                o = h % part_heads * hd
                                f = slice(h * hd, (h + 1) * hd)
                                if kind == "self":
                                    mm = nc.tensor.matmul(ps[0:N, o:o + hd], probT[0:N, n % 2, k * N:(k + 1) * N],
                                                          v_self[:, b, f], start=True, stop=True)
                                else:
                                    for t, (_, mn) in enumerate(MCH):
                                        mm = nc.tensor.matmul(ps[0:N, o:o + hd], probT[0:mn, n % 2, t * N:(t + 1) * N],
                                                              vc[0:mn, b, t, f], start=(t == 0), stop=(t == NM - 1))
                            if (g + 1) % part_groups == 0:
                                mm.then_inc(tok_ready, 1)

                def attention_to_features():
                    before = toks.n - PAIR * parts
                    for b in range(PAIR):
                        for h in range(parts):
                            ps = take()
                            pe.wait_ge(tok_out, toks.at(2 + before + b * parts + h + 1))
                            for c in range(part_chunks):
                                f = (h * part_chunks + c) * P
                                mm = nc.tensor.transpose(ps[:, c * N:(c + 1) * N], o_tok[:, b, f:f + P], ident[0:N, 0:N])
                            mm.then_inc(lin_ready, 1)

                def to_rows(name, per_seq, src, wt, chunks):
                    for b in range(PAIR):
                        ps = free_tok()
                        if per_seq:
                            evicted(name, (b + 1) * per_seq - 1)
                        for c in range(chunks):
                            if not per_seq and b == 0:
                                evicted(name, c)
                            mm = nc.tensor.matmul(ps[0:N, 0:D], src[:, c, b * N:(b + 1) * N], wt[:, c, :],
                                                  start=(c == 0), stop=(c == chunks - 1))
                        mm.then_inc(tok_ready, 1)

                for wt in (w_q, w_k):
                    for m in range(cw):
                        project(wt, m, hT0, T, C)
                fill(take, PLACES["first"])
                evicted("k", cw - 1)
                if L == 0:
                    pe.wait_ge(q_ready, i * QREADY + cw)
                else:
                    pe.wait_ge(q_masked, i * (2 * cw // ROT) + cw // ROT)
                attend("self", {NEXT_ROWS[L][2]: lambda: normalised_to_features(take, i * 6 + 3)})
                attention_to_features()
                to_rows("o1", parts, oT, w["o"], cw)
                evicted("next_t", C - 1)
                fill(take, PLACES["b2_t"])
                normalised_to_features(take, i * 6 + 5)
                if L == 1:
                    pe.sem_inc(ctx_free, 1)
                fill(take, PLACES["b2_q"])
                evicted("t1", C - 1)
                for m in range(cw):
                    project(w["cq"], m, hT, T, C)
                fill(take, PLACES["b2_s"])
                evicted("cv", len(ctx_values) - 1)
                if L == 0:
                    pe.sem_inc(ctx_free, 1)
                    pe.wait_ge(halves_ready, i * (PAIR * cw) + PAIR * cw)
                else:
                    pe.wait_ge(q_masked, i * (2 * cw // ROT) + (cw // ROT + MASKED_PAIRS))
                if L == 1:
                    next_context = {NEXT_CONTEXT["features"] + k:
                                    lambda k=k: context_to_features(take, k, i * (PAIR * NM) + 2 * PAIR * NM)
                                    for k in range(PAIR * CC)}
                else:
                    next_context = {GROUPS_OF["cross"] - 1:
                                    lambda: pe.wait_ge(ctx_loaded, i * (16 * ctx_dmas) + 32 * ctx_dmas)}
                attend("cross", next_context)
                attention_to_features()
                if L == 1:
                    pe.sem_inc(cross_done, 1)
                    pe.wait_ge(halves_ready, i * (PAIR * CC) + 2 * PAIR * CC)
                to_rows("o2", parts, oT, w["co"], cw)
                fill(take, PLACES["b3_t"])
                normalised_to_features(take, i * 6 + 7)
                fill(take, PLACES["b3_f1"])
                evicted("t2", C - 1)
                if L == 1:
                    pe.wait_ge(mlp_loaded, i * 32 + 32)
                for m in range(CF):
                    project(w["f1"], m, hT, T, C)
                fill(take, PLACES["b3_f2"])
                to_rows("f1", 0, gT, w["f2"], CF)
                for count in (jobs, toks, groups):
                    count.end()


def chunked(w, p=P):
    return np.ascontiguousarray(w.reshape(-1, p, w.shape[1]).transpose(1, 0, 2))


def rotary_columns(w):
    return w.reshape(w.shape[0], H, 2, 16, 2).transpose(0, 1, 2, 4, 3).reshape(w.shape)


def feature_columns(v, p=P):
    v = v.reshape(-1, p).T
    return np.concatenate([v, np.zeros((P - p, v.shape[1]), v.dtype)]) if p < P else v


def rotary_tables():
    freq = (np.float32(1.0) / np.float32(10000.0) ** (np.arange(0, 64, 2, dtype=np.float32) / np.float32(64))).astype(np.float32)
    angle = np.arange(M, dtype=np.float32)[:, None] * freq[None, :]
    row = np.arange(P)
    f = 16 * (row % 64 // 32) + row % 16
    sign = np.where(row % 32 < 16, 1.0, -1.0).astype(np.float32)[:, None]
    return np.cos(angle)[:, f].T.astype(np.float32), (np.sin(angle)[:, f].T * sign).astype(np.float32)


def kernel(**inputs):
    import concourse.bacc as bacc
    from concourse.bass_utils import run_bass_kernel_spmd

    v = {k: np.asarray(x) for k, x in inputs.items()}
    l0 = {k[9:]: x for k, x in v.items() if k.startswith("L0_xcond_")}
    l1 = {k[9:]: x for k, x in v.items() if k.startswith("L1_xcond_")}
    cos, sin = rotary_tables()
    mask = np.kron(np.eye(P // HD[0], dtype=np.float32), np.ones((HD[0], 1), np.float32))
    vectors = {
        "b_ada": [l0["b_ada"]], "b_qkv": [l0["b_qkv"]], "b_ctx": [l0["b_ctx"]], "b_fc1_0": [l0["b_fc1"]],
        "b_fc1_1": [l1["ff_b1"]], "ln_w": [l1["ln1_w"], l1["ln2_w"]], "ln_b": [l1["ln1_b"], l1["ln2_b"]],
        "g_b": [l1["g1_b"], l1["g2_b"]], "beta_b": [l1["b1_b"], l1["b2_b"]],
    }
    cols = [feature_columns(x) for name, _ in COLS[:9] for x in vectors[name]]
    cols += [feature_columns(l1["ca_lnc_w"], KC), feature_columns(l1["ca_lnc_b"], KC), mask]
    arrays = {
        "x": v["x"], "ctx": v["ctx_768"],
        "ctxT": v["ctx_768"].reshape(B, M, CC, KC).transpose(0, 3, 2, 1),
        "condT": chunked(v["cond_1024"].T), "cols": np.concatenate(cols, axis=1),
        "rows": np.stack([l0["b_proj"], l0["b_out"], l0["b_fc2"], l1["sa_bo"], l1["ca_bo"], l1["ff_b2"]]).reshape(2, ROWS, D),
        "ident": np.eye(P, dtype=np.float32), "cos": cos, "sin": sin,
        "wada": chunked(l0["W_ada"]),
        "wmod": np.stack([chunked(l1[n]) for n in ("g1_w", "b1_w", "g2_w", "b2_w")], axis=1),
        "wctxT": chunked(l0["W_ctx"].T), "w0_k": chunked(l0["W_k"]), "w0_v": chunked(l0["W_v"]),
        "w0_qkv": chunked(l0["W_qkv"]), "w0_o": chunked(l0["W_proj"]), "w0_cq": chunked(l0["W_q"]),
        "w0_co": chunked(l0["W_out"]), "w0_f1": chunked(l0["W_fc1"]), "w0_f2": chunked(l0["W_fc2"]),
        "w1_q": chunked(rotary_columns(l1["sa_wq"])), "w1_k": chunked(rotary_columns(l1["sa_wkv"][:, :WIDTH[1]])),
        "w1_v": chunked(l1["sa_wkv"][:, WIDTH[1]:]), "w1_o": chunked(l1["sa_wo"]),
        "w1_cq": chunked(rotary_columns(l1["ca_wq"])), "w1_ck": chunked(rotary_columns(l1["ca_wkv"][:, :WIDTH[1]]), KC),
        "w1_cv": chunked(l1["ca_wkv"][:, WIDTH[1]:], KC), "w1_co": chunked(l1["ca_wo"]),
        "w1_f1": chunked(l1["ff_w1"]), "w1_f2": chunked(l1["ff_w2"]),
    }
    nc = bacc.Bacc("TRN2", target_bir_lowering=False, num_devices=1)
    args = {}
    for name in arrays:
        arrays[name] = np.ascontiguousarray(arrays[name])
        args[name] = nc.dram_tensor("in_" + name, arrays[name].shape, F32, kind="ExternalInput").ap()
    out = nc.dram_tensor("out", [B, N, D], F32, kind="ExternalOutput").ap()
    two_blocks(nc, args, out)
    return run_bass_kernel_spmd(nc, [{"in_" + n: x for n, x in arrays.items()}], core_ids=[0]).results[0]["out"]
```
